# Optimizing a Trainium2 kernel written in Bass

```python
import numpy as np
import jax
import jax.numpy as jnp

def _softmax(x, axis=-1):
    return jax.nn.softmax(x, axis=axis)

def _gelu(x):
    return jax.nn.gelu(x, approximate=True)

def _silu(x):
    return jax.nn.silu(x)

def _sigmoid(x):
    return jax.nn.sigmoid(x)

def _layernorm(x, axis=-1, eps=1e-05):
    m = jnp.mean(x, axis=axis, keepdims=True)
    v = jnp.var(x, axis=axis, keepdims=True)
    return (x - m) / jnp.sqrt(v + eps)

def _scatter_add(tgt, idx, src, axis=0):
    return tgt.at[idx].add(src)

def _segment_sum(src, seg, n):
    return jax.ops.segment_sum(src, seg, n)
kernel_name = 'mk_seq_preln_d1_jaxref_r8_fcafa1'

def setup_inputs(seed: int=0):
    np.random.seed(seed)
    _w = jnp.asarray

    def _L0_attn_setup():
        import jax, jax.numpy as jnp
        import numpy as np
        B, S, D = (4, 512, 128)
        CHUNK = 64
        MAX_LR = 0.2
        MIN_DECAY = 0.5
        MAX_NORM = 30.0
        NORM_EPS = 1e-05

        def _forward(x, M_init, eta_w, eta_b, alpha_w, alpha_b, gate_w, gate_b, vg_w1, vg_w2):
            b, s, d = x.shape
            n_ch = s // CHUNK

            def value_gen(y):
                h = jax.nn.silu(y @ vg_w1.T) @ vg_w2.T
                return h + y
            x_chunks = x.reshape(b, n_ch, CHUNK, d).transpose(1, 0, 2, 3)
            M0 = jnp.broadcast_to(M_init, (b, d, d))

            def step(M, chunk):
                eta_tok = jax.nn.sigmoid(chunk @ eta_w + eta_b[0]) * MAX_LR
                alpha_tok = MIN_DECAY + jax.nn.sigmoid(chunk @ alpha_w + alpha_b[0]) * (1.0 - MIN_DECAY)
                eta = eta_tok.mean(axis=1)[:, None, None]
                alpha = alpha_tok.mean(axis=1)[:, None, None]
                outputs = jnp.einsum('bci,boi->bco', chunk, M)
                nrm = jnp.sqrt(jnp.sum(chunk * chunk, axis=-1, keepdims=True))
                keys = chunk / jnp.maximum(nrm, NORM_EPS)
                k_mean = keys.mean(axis=1)
                v_target = value_gen(outputs).mean(axis=1)
                Mk = jnp.einsum('boi,bi->bo', M, k_mean)
                err = v_target - Mk
                update = err[:, :, None] * k_mean[:, None, :]
                M_new = alpha * M + eta * update
                gate = jax.nn.sigmoid(k_mean @ gate_w + gate_b[0])[:, None, None]
                M_new = gate * M_new + (1.0 - gate) * M
                M_norm = jnp.sqrt(jnp.sum(M_new * M_new, axis=(-2, -1), keepdims=True))
                scale = jnp.minimum(MAX_NORM / (M_norm + 1e-06), 1.0)
                return (M_new * scale, outputs)
            M_final, outs = jax.lax.scan(step, M0, x_chunks)
            outs = outs.transpose(1, 0, 2, 3).reshape(b, s, d)
            final_out = value_gen(outs)
            return (final_out, M_final)

        def _reference_tuple_inner(x, M_init, eta_w, eta_b, alpha_w, alpha_b, gate_w, gate_b, vg_w1, vg_w2):
            return _forward(x, M_init, eta_w, eta_b, alpha_w, alpha_b, gate_w, gate_b, vg_w1, vg_w2)
        key = jax.random.key(seed)
        ks = jax.random.split(key, 10)
        return {'x': jax.random.normal(ks[0], (B, S, D), jnp.float32), 'M_init': jax.random.normal(ks[1], (D, D), jnp.float32) * 0.02, 'eta_w': jax.random.normal(ks[2], (D,), jnp.float32) * 0.02, 'eta_b': jax.random.normal(ks[3], (1,), jnp.float32), 'alpha_w': jax.random.normal(ks[4], (D,), jnp.float32) * 0.02, 'alpha_b': jax.random.normal(ks[5], (1,), jnp.float32), 'gate_w': jax.random.normal(ks[6], (D,), jnp.float32) * 0.02, 'gate_b': jax.random.normal(ks[7], (1,), jnp.float32), 'vg_w1': jax.random.normal(ks[8], (D, D), jnp.float32) * 0.02, 'vg_w2': jax.random.normal(ks[9], (D, D), jnp.float32) * 0.02}
    _L0_attn_in = _L0_attn_setup()

    def _L0_ffn_setup():
        import jax, jax.numpy as jnp
        import numpy as np
        D_MODEL = 128
        N_HEAD = 16
        HEAD_DIM = D_MODEL // N_HEAD
        D_FF = 512
        N_EXPERTS = 4
        EPS = 1e-05

        def _layer_norm(x, gamma, beta):
            mu = jnp.mean(x, axis=-1, keepdims=True)
            var = jnp.mean((x - mu) ** 2, axis=-1, keepdims=True)
            return (x - mu) / jnp.sqrt(var + EPS) * gamma + beta
        key = jax.random.key(seed)
        ks = jax.random.split(key, 20)
        f32 = jnp.float32
        sc = 1.0 / np.sqrt(D_MODEL)
        scf = 1.0 / np.sqrt(D_FF)
        return {'src': jax.random.normal(ks[0], (4, 64, D_MODEL), f32), 'Wq': jax.random.normal(ks[1], (D_MODEL, D_MODEL), f32) * sc, 'bq': jnp.zeros((D_MODEL,), f32), 'Wk': jax.random.normal(ks[2], (D_MODEL, D_MODEL), f32) * sc, 'bk': jnp.zeros((D_MODEL,), f32), 'Wv': jax.random.normal(ks[3], (D_MODEL, D_MODEL), f32) * sc, 'bv': jnp.zeros((D_MODEL,), f32), 'Wo': jax.random.normal(ks[4], (D_MODEL, D_MODEL), f32) * sc, 'bo': jnp.zeros((D_MODEL,), f32), 'router_w': jax.random.normal(ks[5], (D_MODEL, 1), f32) * 0.05, 'router_b': jnp.zeros((1,), f32), 'W1': jax.random.normal(ks[6], (N_EXPERTS, D_MODEL, D_FF), f32) * sc, 'b1': jnp.zeros((N_EXPERTS, D_FF), f32), 'W2': jax.random.normal(ks[7], (N_EXPERTS, D_FF, D_MODEL), f32) * scf, 'b2': jnp.zeros((N_EXPERTS, D_MODEL), f32), 'ln1_g': jnp.ones((D_MODEL,), f32), 'ln1_b': jnp.zeros((D_MODEL,), f32), 'ln2_g': jnp.ones((D_MODEL,), f32), 'ln2_b': jnp.zeros((D_MODEL,), f32)}
    _L0_ffn_in = _L0_ffn_setup()
    _d = {'L0_attn_x': _L0_attn_in['x'], 'L0_attn_M_init': _L0_attn_in['M_init'], 'L0_attn_eta_w': _L0_attn_in['eta_w'], 'L0_attn_eta_b': _L0_attn_in['eta_b'], 'L0_attn_alpha_w': _L0_attn_in['alpha_w'], 'L0_attn_alpha_b': _L0_attn_in['alpha_b'], 'L0_attn_gate_w': _L0_attn_in['gate_w'], 'L0_attn_gate_b': _L0_attn_in['gate_b'], 'L0_attn_vg_w1': _L0_attn_in['vg_w1'], 'L0_attn_vg_w2': _L0_attn_in['vg_w2'], 'L0_ffn_Wq': _L0_ffn_in['Wq'], 'L0_ffn_bq': _L0_ffn_in['bq'], 'L0_ffn_Wk': _L0_ffn_in['Wk'], 'L0_ffn_bk': _L0_ffn_in['bk'], 'L0_ffn_Wv': _L0_ffn_in['Wv'], 'L0_ffn_bv': _L0_ffn_in['bv'], 'L0_ffn_Wo': _L0_ffn_in['Wo'], 'L0_ffn_bo': _L0_ffn_in['bo'], 'L0_ffn_router_w': _L0_ffn_in['router_w'], 'L0_ffn_router_b': _L0_ffn_in['router_b'], 'L0_ffn_W1': _L0_ffn_in['W1'], 'L0_ffn_b1': _L0_ffn_in['b1'], 'L0_ffn_W2': _L0_ffn_in['W2'], 'L0_ffn_b2': _L0_ffn_in['b2'], 'L0_ffn_ln1_g': _L0_ffn_in['ln1_g'], 'L0_ffn_ln1_b': _L0_ffn_in['ln1_b'], 'L0_ffn_ln2_g': _L0_ffn_in['ln2_g'], 'L0_ffn_ln2_b': _L0_ffn_in['ln2_b']}
    _x0 = _d['L0_attn_x']
    _d['L0_attn_x'] = jax.random.normal(jax.random.fold_in(jax.random.key(seed), 1), (16, 512, 128), dtype=_x0.dtype)
    del _x0
    return _d

def reference(L0_attn_x, L0_attn_M_init, L0_attn_eta_w, L0_attn_eta_b, L0_attn_alpha_w, L0_attn_alpha_b, L0_attn_gate_w, L0_attn_gate_b, L0_attn_vg_w1, L0_attn_vg_w2, L0_ffn_Wq, L0_ffn_bq, L0_ffn_Wk, L0_ffn_bk, L0_ffn_Wv, L0_ffn_bv, L0_ffn_Wo, L0_ffn_bo, L0_ffn_router_w, L0_ffn_router_b, L0_ffn_W1, L0_ffn_b1, L0_ffn_W2, L0_ffn_b2, L0_ffn_ln1_g, L0_ffn_ln1_b, L0_ffn_ln2_g, L0_ffn_ln2_b):

    def _L0_attn_ref(x, M_init, eta_w, eta_b, alpha_w, alpha_b, gate_w, gate_b, vg_w1, vg_w2):
        import jax, jax.numpy as jnp
        import numpy as np
        B, S, D = (4, 512, 128)
        CHUNK = 64
        MAX_LR = 0.2
        MIN_DECAY = 0.5
        MAX_NORM = 30.0
        NORM_EPS = 1e-05

        def _forward(x, M_init, eta_w, eta_b, alpha_w, alpha_b, gate_w, gate_b, vg_w1, vg_w2):
            b, s, d = x.shape
            n_ch = s // CHUNK

            def value_gen(y):
                h = jax.nn.silu(y @ vg_w1.T) @ vg_w2.T
                return h + y
            x_chunks = x.reshape(b, n_ch, CHUNK, d).transpose(1, 0, 2, 3)
            M0 = jnp.broadcast_to(M_init, (b, d, d))

            def step(M, chunk):
                eta_tok = jax.nn.sigmoid(chunk @ eta_w + eta_b[0]) * MAX_LR
                alpha_tok = MIN_DECAY + jax.nn.sigmoid(chunk @ alpha_w + alpha_b[0]) * (1.0 - MIN_DECAY)
                eta = eta_tok.mean(axis=1)[:, None, None]
                alpha = alpha_tok.mean(axis=1)[:, None, None]
                outputs = jnp.einsum('bci,boi->bco', chunk, M)
                nrm = jnp.sqrt(jnp.sum(chunk * chunk, axis=-1, keepdims=True))
                keys = chunk / jnp.maximum(nrm, NORM_EPS)
                k_mean = keys.mean(axis=1)
                v_target = value_gen(outputs).mean(axis=1)
                Mk = jnp.einsum('boi,bi->bo', M, k_mean)
                err = v_target - Mk
                update = err[:, :, None] * k_mean[:, None, :]
                M_new = alpha * M + eta * update
                gate = jax.nn.sigmoid(k_mean @ gate_w + gate_b[0])[:, None, None]
                M_new = gate * M_new + (1.0 - gate) * M
                M_norm = jnp.sqrt(jnp.sum(M_new * M_new, axis=(-2, -1), keepdims=True))
                scale = jnp.minimum(MAX_NORM / (M_norm + 1e-06), 1.0)
                return (M_new * scale, outputs)
            M_final, outs = jax.lax.scan(step, M0, x_chunks)
            outs = outs.transpose(1, 0, 2, 3).reshape(b, s, d)
            final_out = value_gen(outs)
            return (final_out, M_final)

        def _reference_tuple_inner(x, M_init, eta_w, eta_b, alpha_w, alpha_b, gate_w, gate_b, vg_w1, vg_w2):
            return _forward(x, M_init, eta_w, eta_b, alpha_w, alpha_b, gate_w, gate_b, vg_w1, vg_w2)
        return _reference_tuple_inner(x, M_init, eta_w, eta_b, alpha_w, alpha_b, gate_w, gate_b, vg_w1, vg_w2)[0]

    def _L0_ffn_ref(src, Wq, bq, Wk, bk, Wv, bv, Wo, bo, router_w, router_b, W1, b1, W2, b2, ln1_g, ln1_b, ln2_g, ln2_b):
        import jax, jax.numpy as jnp
        import numpy as np
        D_MODEL = 128
        N_HEAD = 16
        HEAD_DIM = D_MODEL // N_HEAD
        D_FF = 512
        N_EXPERTS = 4
        EPS = 1e-05

        def _layer_norm(x, gamma, beta):
            mu = jnp.mean(x, axis=-1, keepdims=True)
            var = jnp.mean((x - mu) ** 2, axis=-1, keepdims=True)
            return (x - mu) / jnp.sqrt(var + EPS) * gamma + beta
        B, T, _ = src.shape
        q = (src @ Wq + bq).reshape(B, T, N_HEAD, HEAD_DIM)
        k = (src @ Wk + bk).reshape(B, T, N_HEAD, HEAD_DIM)
        v = (src @ Wv + bv).reshape(B, T, N_HEAD, HEAD_DIM)
        scale = HEAD_DIM ** (-0.5)
        scores = jnp.einsum('bqhd,bkhd->bhqk', q, k) * scale
        probs = jax.nn.softmax(scores, axis=-1)
        attn = jnp.einsum('bhqk,bkhd->bqhd', probs, v).reshape(B, T, D_MODEL)
        attn = attn @ Wo + bo
        x = _layer_norm(src + attn, ln1_g, ln1_b)
        keys = (x @ router_w + router_b)[..., 0]
        expert_idx = jnp.remainder(jnp.floor(keys).astype(jnp.int32), N_EXPERTS)
        ff_out = jnp.zeros_like(x)
        for e in range(N_EXPERTS):
            h = jax.nn.relu(x @ W1[e] + b1[e])
            y = h @ W2[e] + b2[e]
            ff_out = ff_out + jnp.where((expert_idx == e)[..., None], y, 0.0)
        return _layer_norm(x + ff_out, ln2_g, ln2_b)
    x = L0_attn_x
    x = x + _L0_attn_ref(_layernorm(x, axis=-1), L0_attn_M_init, L0_attn_eta_w, L0_attn_eta_b, L0_attn_alpha_w, L0_attn_alpha_b, L0_attn_gate_w, L0_attn_gate_b, L0_attn_vg_w1, L0_attn_vg_w2)
    x = x + _L0_ffn_ref(_layernorm(x, axis=-1), L0_ffn_Wq, L0_ffn_bq, L0_ffn_Wk, L0_ffn_bk, L0_ffn_Wv, L0_ffn_bv, L0_ffn_Wo, L0_ffn_bo, L0_ffn_router_w, L0_ffn_router_b, L0_ffn_W1, L0_ffn_b1, L0_ffn_W2, L0_ffn_b2, L0_ffn_ln1_g, L0_ffn_ln1_b, L0_ffn_ln2_g, L0_ffn_ln2_b)
    return x

_drawn_inputs = setup_inputs


def setup_inputs(seed=0):
    import zlib

    import numpy as np

    out = dict(_drawn_inputs(seed))
    spreads = {'L0_ffn_bq': (0.0, 0.1),
     'L0_ffn_bk': (0.0, 2.0),
     'L0_ffn_bv': (0.0, 0.1),
     'L0_ffn_bo': (0.0, 0.1),
     'L0_ffn_b1': (0.0, 0.274),
     'L0_ffn_b2': (0.0, 0.1),
     'L0_ffn_ln1_g': (1.0, 0.2),
     'L0_ffn_ln1_b': (0.0, 0.1),
     'L0_ffn_ln2_g': (1.0, 0.2),
     'L0_ffn_ln2_b': (0.0, 0.1)}
    factors = {'L0_attn_eta_w': 200.0,
     'L0_attn_alpha_w': 131.228,
     'L0_attn_gate_w': 200.0,
     'L0_attn_vg_w1': 3.489,
     'L0_attn_vg_w2': 3.561}
    for name, (base, spread) in spreads.items():
        noise = np.random.default_rng([zlib.crc32(name.encode()), seed]).standard_normal(out[name].shape)
        drawn = base * np.exp(spread * noise) if base else spread * noise
        out[name] = jnp.asarray(drawn.astype(out[name].dtype))
    for name, factor in factors.items():
        out[name] = (out[name] * factor).astype(out[name].dtype)
    return out
```

```python
from collections import namedtuple
from contextlib import ExitStack

import concourse.bass as bass
from concourse import mybir

F32 = mybir.dt.float32
BF16 = mybir.dt.bfloat16
I32 = mybir.dt.int32
ACT = mybir.ActivationFunctionType
ALU = mybir.AluOpType
AX = mybir.AxisListType

P = 128
EPS = 1e-5


_ATTN = ("x", "M_init", "eta_w", "eta_b", "alpha_w", "alpha_b", "gate_w", "gate_b", "vg_w1", "vg_w2")
_FFN = ("Wq", "bq", "Wk", "bk", "Wv", "bv", "Wo", "bo", "router_w", "router_b", "W1", "b1", "W2", "b2",
        "ln1_g", "ln1_b", "ln2_g", "ln2_b")
Inputs = namedtuple("Inputs", _ATTN + _FFN)


def column(ap):
    return ap.rearrange("(p a) -> p a", a=1)


def on_all(ap, n):
    return ap.rearrange("(a n) -> a n", a=1).broadcast_to([P, n])


def memory_program(nc, io, x_tok, vg_t, ident, ones):
    B, S, D = io.x.shape
    TILES = B * S // P
    CH = 64
    NCH = S // CH
    HALVES = P // CH
    TPB = S // P
    CW = CH + 1
    G = 2
    GB = B // G
    QUARTERS = 4
    TQ = TILES // QUARTERS

    with ExitStack() as ctx:
        def sb(name, shape, dt=F32):
            return ctx.enter_context(nc.sbuf_tensor(name, shape, dt))

        def sem(name):
            return ctx.enter_context(nc.semaphore(name))

        xhat = sb("xhat", [P, B, NCH, CW])
        key = sb("key", [P, B, NCH])
        mt = sb("mt", [P, B, D])
        coef_keep = sb("coef_keep", [P, NCH, B])
        coef_err = sb("coef_err", [P, NCH, B])
        w1t = sb("w1t", [P, D])
        w2t = sb("w2t", [P, D])
        minit_t = sb("minit_t", [P, D])

        with ExitStack() as c2:
            def sb2(name, shape, dt=F32):
                return c2.enter_context(nc.sbuf_tensor(name, shape, dt))

            def sem2(name):
                return c2.enter_context(nc.semaphore(name))

            xn = sb2("xn", [P, 2, TPB, D])
            stats = sb2("stats", [P, TILES, 6])
            meanvar = sb2("meanvar", [P, TILES, 2])
            vareps = sb2("vareps", [P, TILES])
            rstd = sb2("rstd", [P, TILES])
            neghalf = sb2("neghalf", [P, TILES])
            sumsq = sb2("sumsq", [P, TILES])
            sqdump = sb2("sqdump", [P, 2, D])
            kinv = sb2("kinv", [P, TILES])
            halfmask = sb2("halfmask", [P, HALVES])
            key_w = sb2("key_w", [P, TILES, 2, HALVES])
            vecs = sb2("vecs", [P, 3])
            wrep = sb2("wrep", [P, 3, P])
            biases = sb2("biases", [P, 3])
            raw_w = sb2("raw_w", [P, 3, D])
            sig = sb2("sig", [P, 2, 2, S])
            sig_sum = sb2("sig_sum", [P, 2, 2, NCH])
            gate = sb2("gate", [P, B, NCH])
            alpha = sb2("alpha", [P, B, NCH])
            eta = sb2("eta", [P, B, NCH])
            xnk = sb2("xnk", [P, TILES, D])
            ps_t = c2.enter_context(nc.psum_tensor("ps_t", [P, 2, S], F32))
            ps_g = c2.enter_context(nc.psum_tensor("ps_g", [P, 2, 2, S], F32))
            ps_k = c2.enter_context(nc.psum_tensor("ps_k", [P, 512], F32))
            ps_w = c2.enter_context(nc.psum_tensor("ps_w", [P, 4, P], F32))

            x_in = [sem2(f"x_in{q}") for q in range(QUARTERS)]
            w_in = sem2("w_in")
            consts = sem2("consts")
            stat_done = sem2("stat_done")
            mean_done = sem2("mean_done")
            vareps_done = sem2("vareps_done")
            rstd_done = sem2("rstd_done")
            xn_done = sem2("xn_done")
            sumsq_done = sem2("sumsq_done")
            kclamp_done = sem2("kclamp_done")
            kinv_done = sem2("kinv_done")
            key_w_done = sem2("key_w_done")
            t_done = sem2("t_done")
            xhat_done = sem2("xhat_done")
            wt_done = sem2("wt_done")
            wt_copied = sem2("wt_copied")
            wrep_done = sem2("wrep_done")
            gates_mm = sem2("gates_mm")
            sig_done = sem2("sig_done")
            sigsum_done = sem2("sigsum_done")
            key_mm = sem2("key_mm")
            key_done = sem2("key_done")
            gate_mm = sem2("gate_mm")
            gate_done = sem2("gate_done")
            coef_step = sem2("coef_step")

            block = c2.enter_context(nc.Block())

            def turns(engine, body, n):
                body(0, True)
                with engine.Fori(1, n) as i:
                    body(i, False)

            x_rows = io.x.rearrange("b s d -> (b s) d").rearrange("(i p) d -> p i d", p=P)

            @block.sync
            def _(sp):
                for q in range(QUARTERS):
                    sp.dma_start(x_tok[:, q * TQ:(q + 1) * TQ, :], x_rows[:, q * TQ:(q + 1) * TQ, :]).then_inc(x_in[q], 16)

            @block.scalar
            def _(act):
                for n, w in enumerate((io.M_init, io.vg_w1, io.vg_w2)):
                    act.dma_start(raw_w[:, n, :], w).then_inc(w_in, 16)
                for n, (w, b) in enumerate(((io.eta_w, io.eta_b), (io.alpha_w, io.alpha_b), (io.gate_w, io.gate_b))):
                    act.dma_start(vecs[:, n:n + 1], column(w)).then_inc(w_in, 16)
                    act.dma_start(biases[:, n:n + 1], on_all(b, 1)).then_inc(w_in, 16)
                def squares(b, first):
                    act.wait_ge(xn_done, b + 1)
                    for j in range(TPB):
                        if j == 0 and not first:
                            act.wait_ge(sumsq_done, TPB * b)
                        if j >= 2:
                            act.wait_ge(sumsq_done, TPB * b + j - 1)
                        act.activation(sqdump[:, j % 2, :], xnk[:, bass.ds(b * TPB + j, 1), :], ACT.Square,
                                       accum_out=sumsq[:, bass.ds(b * TPB + j, 1)]).then_inc(sumsq_done, 1)

                turns(nc.scalar, squares, B)
                act.wait_ge(w_in, 16 * 9)
                def sigmoids(h, first):
                    for r in range(2):
                        act.wait_ge(gates_mm, (h * 2 + r) * 2 + 2)
                        if r == 0 and not first:
                            act.wait_ge(sigsum_done, h * 4)
                        for n in range(2):
                            act.activation(sig[:, r, n, :], ps_g[:, r, n, :], ACT.Sigmoid,
                                           bias=biases[:, n:n + 1]).then_inc(sig_done, 1)

                turns(nc.scalar, sigmoids, B // 2)
                act.wait_ge(gate_mm, 1)
                act.activation(gate[:].rearrange("p b c -> p (b c)"), ps_w[:, 3, :], ACT.Sigmoid,
                               bias=biases[:, 2:3]).then_inc(gate_done, 1)

            @block.gpsimd
            def _(pool):
                pool.memset(ident[:], 0.0).then_inc(consts, 1)
                pool.memset(ones[:], 1.0).then_inc(consts, 1)
                pool.memset(neghalf[:], -0.5).then_inc(consts, 1)
                pool.memset(halfmask[:], 1.0 / CH).then_inc(consts, 1)
                pool.wait_ge(consts, 4)
                pool.affine_select(out=ident[:], in_=ident[:], compare_op=ALU.not_equal, fill=1.0, base=0,
                                   pattern=[[-1, P]], channel_multiplier=1).then_inc(consts, 1)
                pool.affine_select(out=halfmask[:, 0:1], in_=halfmask[:, 0:1], compare_op=ALU.is_ge, fill=0.0,
                                   base=CH - 1, pattern=[[0, 1]], channel_multiplier=-1).then_inc(consts, 1)
                pool.affine_select(out=halfmask[:, 1:2], in_=halfmask[:, 1:2], compare_op=ALU.is_ge, fill=0.0,
                                   base=-CH, pattern=[[0, 1]], channel_multiplier=1).then_inc(consts, 1)
                pool.wait_ge(vareps_done, 1)
                pool.tensor_tensor(rstd[:], vareps[:], neghalf[:], ALU.pow).then_inc(rstd_done, 1)
                pool.wait_ge(kclamp_done, 1)
                pool.tensor_tensor(kinv[:], sumsq[:], neghalf[:], ALU.pow).then_inc(kinv_done, 1)

            @block.tensor
            def _(pe):
                pe.wait_ge(consts, 7)
                pe.wait_ge(w_in, 16 * 9)
                for n in range(3):
                    mm = pe.transpose(ps_w[:, n, :], raw_w[:, n, :], ident[:])
                mm.then_inc(wt_done, 1)
                pe.wait_ge(wrep_done, 3)

                def gates(b, r):
                    pe.wait_ge(xhat_done, b + 1)
                    for n in range(2):
                        pe.matmul(ps_g[:, r, n, :], wrep[:, n, :], xhat[:, bass.ds(b, 1), :, 0:CH],
                                  start=True, stop=True).then_inc(gates_mm, 1)

                def turn(r):
                    for j in range(TPB):
                        mm = pe.transpose(ps_t[:, r, j * P:(j + 1) * P], xn[:, r, j, :], ident[:])
                    mm.then_inc(t_done, 1)

                def pair_turned(h, first):
                    for r in range(2):
                        pe.wait_ge(xn_done, h * 2 + r + 1)
                        if r == 0 and not first:
                            pe.wait_ge(xhat_done, h * 2)
                        turn(r)

                def pair_gates(h, first):
                    for r in range(2):
                        if r == 0 and not first:
                            pe.wait_ge(sig_done, h * 4)
                        gates(h * 2 + r, r)

                turns(nc.tensor, pair_turned, B // 2)
                turns(nc.tensor, pair_gates, B // 2)
                pe.wait_ge(key_w_done, 2)
                for i in range(TILES):
                    mm = pe.matmul(ps_k[:, i * 2 * HALVES:(i + 1) * 2 * HALVES], xnk[:, i, :],
                                   key_w[:, i].rearrange("p k h -> p (k h)"), start=True, stop=True)
                mm.then_inc(key_mm, 1)
                pe.wait_ge(key_done, 1)
                pe.matmul(ps_w[:, 3, :], wrep[:, 2, :], key[:].rearrange("p b c -> p (b c)"), start=True, stop=True).then_inc(gate_mm, 1)

            @block.vector
            def _(dve):
                for q in range(QUARTERS):
                    dve.wait_ge(x_in[q], 16)
                    for i in range(q * TQ, (q + 1) * TQ):
                        dve.bn_stats(stats[:, i, :], x_tok[:, i, :]).then_inc(stat_done, 1)
                    for i in range(q * TQ, (q + 1) * TQ):
                        dve.wait_ge(stat_done, i + 1)
                        dve.bn_aggr(meanvar[:, i, :], stats[:, i, :]).then_inc(mean_done, 1)
                dve.wait_ge(mean_done, TILES)
                dve.tensor_scalar(vareps[:], meanvar[:, :, 1], EPS, None, ALU.add).then_inc(vareps_done, 1)
                dve.wait_ge(wt_done, 1)
                for n, w in enumerate((minit_t, w1t, w2t)):
                    dve.tensor_copy(w[:], ps_w[:, n, :]).then_inc(wt_copied, 1)
                for n in range(3):
                    dve.tensor_scalar(wrep[:, n, :], ones[:], vecs[:, n:n + 1], None, ALU.mult).then_inc(wrep_done, 1)
                dve.wait_ge(rstd_done, 1)

                def normalise(b, r):
                    for j in range(TPB):
                        i = b * TPB + j
                        cp = dve.tensor_scalar(xnk[:, bass.ds(i, 1), :], x_tok[:, bass.ds(i, 1), :],
                                               meanvar[:, bass.ds(i, 1), 0], rstd[:, bass.ds(i, 1)],
                                               ALU.subtract, ALU.mult)
                        last = dve.tensor_scalar(xn[:, r, j, :], x_tok[:, bass.ds(i, 1), :],
                                                 meanvar[:, bass.ds(i, 1), 0], rstd[:, bass.ds(i, 1)],
                                                 ALU.subtract, ALU.mult)
                    last.then_inc(xn_done, 1)

                def spread(b, r):
                    dve.tensor_copy(xhat[:, bass.ds(b, 1), :, 0:CH],
                                    ps_t[:, r, :].rearrange("p (a c t) -> p a c t", a=1, t=CH)).then_inc(xhat_done, 1)

                def gate_sums(b, r):
                    dve.wait_ge(sig_done, 2 * b + 2)
                    for n in range(2):
                        dve.tensor_reduce(sig_sum[:, r, n, :], sig[:, r, n, :].rearrange("p (c t) -> p c t", t=CH),
                                          AX.X, ALU.add).then_inc(sigsum_done, 1)
                    dve.wait_ge(sigsum_done, 2 * b + 2)
                    dve.tensor_scalar(eta[:, bass.ds(b, 1), :], sig_sum[:, r, 0:1, :], 0.2 / CH, None, ALU.mult)\
                       .then_inc(coef_step, 1)
                    dve.tensor_scalar(alpha[:, bass.ds(b, 1), :], sig_sum[:, r, 1:2, :], 0.5 / CH, 0.5, ALU.mult,
                                      ALU.add).then_inc(coef_step, 1)

                def pair_normalised(h, first):
                    if not first:
                        dve.wait_ge(t_done, h * 2)
                    for r in range(2):
                        normalise(h * 2 + r, r)
                    for r in range(2):
                        dve.wait_ge(t_done, h * 2 + r + 1)
                        spread(h * 2 + r, r)

                turns(nc.vector, pair_normalised, B // 2)
                dve.wait_ge(sumsq_done, TILES)
                dve.tensor_scalar(sumsq[:], sumsq[:], 1e-10, None, ALU.max).then_inc(kclamp_done, 1)
                with nc.vector.Fori(0, B // 2) as h:
                    for r in range(2):
                        gate_sums(h * 2 + r, r)
                dve.wait_ge(kinv_done, 1)
                halves = halfmask[:].rearrange("p (a h) -> p a h", a=1).broadcast_to([P, TILES, HALVES])
                dve.tensor_tensor(key_w[:, :, 0, :], kinv[:].rearrange("p (i a) -> p i a", a=1)
                                  .broadcast_to([P, TILES, HALVES]), halves, ALU.mult).then_inc(key_w_done, 1)
                dve.wait_ge(key_w_done, 1)
                dve.tensor_tensor(key_w[:, :, 1, :], halves, key_w[:, :, 0, :], ALU.subtract).then_inc(key_w_done, 1)
                dve.wait_ge(key_mm, 1)
                means = ps_k[:, 0:B * NCH * 2].rearrange("p (b i k h) -> p k b i h", b=B, i=TPB, k=2)
                dve.tensor_copy(key[:].rearrange("p b (i h) -> p b i h", h=HALVES), means[:, 0]).then_inc(key_done, 1)
                dve.tensor_copy(xhat[:, :, :, CH].rearrange("p b (i h) -> p b i h", h=HALVES), means[:, 1])\
                   .then_inc(key_done, 1)
                dve.wait_ge(gate_done, 1)
                dve.wait_ge(coef_step, 2 * B)
                dve.tensor_tensor(coef_err[:].rearrange("p c b -> p b c"), gate[:], eta[:], ALU.mult).then_inc(coef_step, 1)
                dve.tensor_tensor(alpha[:], gate[:], alpha[:], ALU.mult).then_inc(coef_step, 1)
                dve.tensor_scalar(gate[:], gate[:], -1.0, 1.0, ALU.mult, ALU.add).then_inc(coef_step, 1)
                dve.wait_ge(coef_step, 2 * B + 3)
                dve.tensor_tensor(coef_keep[:].rearrange("p c b -> p b c"), gate[:], alpha[:], ALU.add).then_inc(coef_step, 1)

        with ExitStack() as c3:
            def sb3(name, shape, dt=F32):
                return c3.enter_context(nc.sbuf_tensor(name, shape, dt))

            def sems(name):
                return [c3.enter_context(nc.semaphore(f"{name}{g}")) for g in range(G)]

            y = sb3("y", [P, G, GB, CH])
            hid = sb3("hid", [P, G, GB * CH])
            lead = sb3("lead", [P, G, GB])
            hsum = sb3("hsum", [P, G, GB])
            err = sb3("err", [P, G, GB])
            err_s = sb3("err_s", [P, G, GB])
            diag = sb3("diag", [P, G, GB, D])
            mta = sb3("mta", [P, B, D])
            sq = sb3("sq", [P, G, 2, D])
            ssq = sb3("ssq", [P, G, GB])
            norm2 = sb3("norm2", [P, G, GB])
            norm = sb3("norm", [P, G, GB])
            norm_inv = sb3("norm_inv", [P, G, GB])
            scale = sb3("scale", [P, G, GB])
            keep = sb3("keep", [P, G, GB])
            half = sb3("half", [P, GB])
            ps_y = [c3.enter_context(nc.psum_tensor(f"ps_y{g}", [P, 2, 512], F32)) for g in range(G)]
            ps_h = [c3.enter_context(nc.psum_tensor(f"ps_h{g}", [P, 512], F32)) for g in range(G)]
            ps_v = [c3.enter_context(nc.psum_tensor(f"ps_v{g}", [P, 512], F32)) for g in range(G)]
            start_done = c3.enter_context(nc.semaphore("start_done"))
            mt_done, y_mm, y_done, lead_done, h_mm, h_done, hsum_done, hs_mm, v_mm, v_done = (
                sems(n) for n in ("mt_done", "y_mm", "y_done", "lead_done", "h_mm", "h_done", "hsum_done", "hs_mm",
                                  "v_mm", "v_done"))
            err_done, errs_done, diag_done, spread_mm, keep_done, mta_done, ssq_done = (
                sems(n) for n in ("err_done", "errs_done", "diag_done", "spread_mm", "keep_done", "mta_done", "ssq_done"))
            norm_mm, norm_c, norm_done, ninv_a, ninv_b, scale_done = (
                sems(n) for n in ("norm_mm", "norm_c", "norm_done", "ninv_a", "ninv_b", "scale_done"))
            block = c3.enter_context(nc.Block())

            HB = GB // 2

            def y_part(g, lo, hi):
                return ps_y[g][:, :, 0:HB * CW].rearrange("p k (b t) -> p k b t", t=CW)[:, :, :, lo:hi]

            def steps(engine, body):
                body(0, True, False)
                with engine.Fori(1, NCH - 1) as c:
                    body(c, False, False)
                body(NCH - 1, False, True)

            def at(c):
                return slice(c, c + 1) if c.__class__ is int else bass.ds(c, 1)

            @block.tensor
            def _(pe):
                pe.wait_ge(start_done, 2)

                def body(c, first, last):
                    for g in range(G):
                        if not first:
                            pe.wait_ge(mt_done[g], c * GB)
                        for b in range(GB):
                            mm = pe.matmul(ps_y[g][:, b // HB, (b % HB) * CW:(b % HB + 1) * CW], mt[:, g * GB + b, :],
                                           xhat[:, g * GB + b, at(c), :], start=True, stop=True)
                        mm.then_inc(y_mm[g], 1)
                        if not first:
                            pe.wait_ge(ssq_done[g], c * GB)
                            pe.matmul(ps_h[g][:, 0:GB], ones[:], ssq[:, g, :], start=True, stop=True).then_inc(norm_mm[g], 1)
                    for g in range(G):
                        pe.wait_ge(y_done[g], c + 1)
                        pe.matmul(ps_h[g][:], w1t[:], y[:, g].rearrange("p b t -> p (b t)"), start=True, stop=True)\
                          .then_inc(h_mm[g], 1)
                    if not last:
                        for g in range(G):
                            pe.wait_ge(hsum_done[g], c + 1)
                            pe.matmul(ps_h[g][:, 0:GB], w2t[:], hsum[:, g], start=True, stop=True).then_inc(hs_mm[g], 1)

                    def second(g):
                        pe.wait_ge(h_done[g], c + 1)
                        if not first:
                            pe.wait_ge(v_done[g], c)
                        pe.matmul(ps_v[g][:], w2t[:], hid[:, g], start=True, stop=True).then_inc(v_mm[g], 1)

                    def spread(g):
                        pe.wait_ge(diag_done[g], c + 1)
                        for k in range(2):
                            mm = pe.matmul(ps_y[g][:, k, :], ones[:],
                                           diag[:, g, k * HB:(k + 1) * HB, :].rearrange("p b d -> p (b d)"),
                                           start=True, stop=True)
                            mm.then_inc(spread_mm[g], 1)

                    second(0)
                    if not last:
                        spread(0)
                        spread(1)
                    second(1)

                steps(nc.tensor, body)

            @block.scalar
            def _(act):
                def body(c, first, last):
                    if not first:
                        for g in range(G):
                            for b in range(GB):
                                act.wait_ge(mt_done[g], c * GB + (b + 1 - GB))
                                if b >= 2:
                                    act.wait_ge(ssq_done[g], c * GB + (b - 1 - GB))
                                act.activation(sq[:, g, b % 2, :], mt[:, g * GB + b, :], ACT.Square,
                                               accum_out=ssq[:, g, b:b + 1]).then_inc(ssq_done[g], 1)
                    for g in range(G):
                        act.wait_ge(h_mm[g], c + 1)
                        if not first:
                            act.wait_ge(v_mm[g], c)
                        act.activation(hid[:, g], ps_h[g][:], ACT.Silu).then_inc(h_done[g], 1)

                steps(nc.scalar, body)

            @block.gpsimd
            def _(pool):
                pool.memset(half[:], 0.5).then_inc(start_done, 1)

                def body(c, first, last):
                    if not first:
                        for g in range(G):
                            pool.wait_ge(norm_c[g], c)
                            pool.tensor_tensor(norm[:, g], norm2[:, g], half[:], ALU.pow).then_inc(norm_done[g], 1)
                    for g in range(G):
                        if last:
                            continue
                        if not first:
                            pool.wait_ge(scale_done[g], c)
                            pool.tensor_tensor(keep[:, g:g + 1], coef_keep[:, at(c), g * GB:(g + 1) * GB], scale[:, g:g + 1],
                                               ALU.mult).then_inc(keep_done[g], 1)
                            pool.wait_ge(keep_done[g], c)
                            factor = keep[:, g]
                        else:
                            pool.wait_ge(start_done, 2)
                            factor = coef_keep[:, 0, g * GB:(g + 1) * GB]
                        pool.tensor_tensor(mta[:, g * GB:(g + 1) * GB, :], mt[:, g * GB:(g + 1) * GB, :],
                                           factor.rearrange("p (b a) -> p b a", a=1).broadcast_to([P, GB, D]),
                                           ALU.mult).then_inc(mta_done[g], 1)

                pool.wait_ge(start_done, 1)
                steps(nc.gpsimd, body)

            @block.vector
            def _(dve):
                dve.wait_ge(start_done, 1)
                dve.tensor_copy(mt[:], minit_t[:].rearrange("p (a d) -> p a d", a=1).broadcast_to([P, B, D]))\
                   .then_inc(start_done, 1)

                def body(c, first, last):
                    if not first:
                        for g in range(G):
                            dve.wait_ge(norm_mm[g], c)
                            dve.tensor_copy(norm2[:, g], ps_h[g][:, 0:GB]).then_inc(norm_c[g], 1)
                    for g in range(G):
                        if not first:
                            dve.wait_ge(norm_done[g], c)
                            dve.tensor_scalar(norm_inv[:, g], norm[:, g], 1e-6, None, ALU.add).then_inc(ninv_a[g], 1)
                            dve.wait_ge(ninv_a[g], c)
                            dve.reciprocal(norm_inv[:, g], norm_inv[:, g]).then_inc(ninv_b[g], 1)
                            dve.wait_ge(ninv_b[g], c)
                            dve.tensor_scalar(scale[:, g], norm_inv[:, g], 30.0, 1.0, ALU.mult, ALU.min)\
                               .then_inc(scale_done[g], 1)
                        dve.wait_ge(y_mm[g], c + 1)
                        out_y = y[:, g].rearrange("p (k b) t -> p k b t", k=2)
                        out_lead = lead[:, g].rearrange("p (k b a) -> p k b a", k=2, a=1)
                        if first:
                            dve.tensor_copy(out_y, y_part(g, 0, CH)).then_inc(y_done[g], 1)
                            dve.tensor_copy(out_lead, y_part(g, CH, CW)).then_inc(lead_done[g], 1)
                        else:
                            dve.wait_ge(scale_done[g], c)
                            s = scale[:, g].rearrange("p (k b a) -> p k b a", k=2, a=1)
                            dve.tensor_tensor(out_y, y_part(g, 0, CH), s.broadcast_to([P, 2, HB, CH]), ALU.mult)\
                               .then_inc(y_done[g], 1)
                            dve.tensor_tensor(out_lead, y_part(g, CH, CW), s, ALU.mult).then_inc(lead_done[g], 1)

                    def error(g):
                        dve.wait_ge(hs_mm[g], c + 1)
                        dve.wait_ge(lead_done[g], c + 1)
                        dve.scalar_tensor_tensor(out=err[:, g], in0=ps_h[g][:, 0:GB], scalar=1.0 / CH, in1=lead[:, g],
                                                 op0=ALU.mult, op1=ALU.add).then_inc(err_done[g], 1)
                        dve.wait_ge(err_done[g], c + 1)
                        dve.tensor_tensor(err_s[:, g:g + 1], err[:, g:g + 1], coef_err[:, at(c), g * GB:(g + 1) * GB],
                                          ALU.mult).then_inc(errs_done[g], 1)
                        dve.wait_ge(errs_done[g], c + 1)
                        dve.tensor_tensor(diag[:, g], ident[:].rearrange("p (a d) -> p a d", a=1).broadcast_to([P, GB, D]),
                                          err_s[:, g].rearrange("p (b a) -> p b a", a=1).broadcast_to([P, GB, D]),
                                          ALU.mult).then_inc(diag_done[g], 1)

                    def outputs(g):
                        dve.wait_ge(v_mm[g], c + 1)
                        dve.wait_ge(y_done[g], c + 1)
                        dve.tensor_tensor(vg_t[:, g * GB:(g + 1) * GB, bass.ds(c * CH, CH)],
                                          ps_v[g][:].rearrange("p (b t) -> p b t", t=CH), y[:, g], ALU.add)\
                           .then_inc(v_done[g], 1)

                    def update(g):
                        dve.wait_ge(mta_done[g], c + 1)
                        if not first:
                            dve.wait_ge(ssq_done[g], c * GB)
                        for b in range(GB):
                            if b % HB == 0:
                                dve.wait_ge(spread_mm[g], c * 2 + (b // HB + 1))
                            dve.scalar_tensor_tensor(
                                out=mt[:, g * GB + b, :], in0=ps_y[g][:, b // HB, (b % HB) * D:(b % HB + 1) * D],
                                scalar=key[:, g * GB + b, at(c)], in1=mta[:, g * GB + b, :],
                                op0=ALU.mult, op1=ALU.add).then_inc(mt_done[g], 1)

                    if not last:
                        for g in range(G):
                            dve.wait_ge(h_done[g], c + 1)
                            dve.tensor_reduce(hsum[:, g], hid[:, g].rearrange("p (b t) -> p b t", t=CH), AX.X, ALU.add)\
                               .then_inc(hsum_done[g], 1)
                        error(0)
                        error(1)
                    outputs(0)
                    if not last:
                        update(0)
                        update(1)
                    outputs(1)

                steps(nc.vector, body)


def attention_program(nc, io, x_tok, vg_t, ident, ones, rows_dram, SEG, row_w, count, passed_by):
    B, S, D = io.x.shape
    H = 16
    HD = D // H
    SCALE = HD ** -0.5
    T = S // P
    PAIRS = H // 2
    QUADS = H // 4
    TERMS = 6
    HROWS = TERMS * HD
    PROWS = 2 * HROWS
    SHIFTS = 3
    KROWS = PROWS + 2 * SHIFTS
    Q_PARTS = (0, 0, 1, 0, 1, 2)
    K_PARTS = (1, 0, 0, 2, 1, 0)
    SLOTS = 32
    UNITS = 64
    VW = 32
    RING = 4
    E = io.W1.shape[0]

    MISC = (("mx1", 1, 0), ("vg", 3, 2), ("o3", 5, -1), ("at", 7, -1), ("z", 9, 2), ("wo", 10, -1), ("q", 12, 2),
            ("k", 13, 2), ("o0", 14, 0), ("v", 16, 2), ("mx0", 18, 1), ("o1", 21, 0), ("rk", 26, -1), ("o2", 29, 0))
    MIDDLE = 16
    LOOP_FROM, LOOP_TO = 2, 14
    FIRST, LAST = -2, B

    def valid(i, d):
        return 0 <= i + d < B

    def uses_before(i, name):
        order = [n for n, _, _ in MISC]
        if i.__class__ is int:
            n = sum(valid(k, d) for k in range(FIRST, i) for _, _, d in MISC)
            return n + sum(valid(i, d) for _, _, d in MISC[:order.index(name)])
        return i * len(MISC) + (uses_before(LOOP_FROM, MISC[0][0]) + order.index(name) - LOOP_FROM * len(MISC))

    def used(i, name):
        if i.__class__ is int and not valid(i, [d for n, _, d in MISC if n == name][0]):
            return 0
        return uses_before(i, name) + 1

    def slot_of(name):
        return [s for n, s, _ in MISC if n == name][0]

    def wait(engine, semaphore, value):
        if value.__class__ is not int or value > 0:
            engine.wait_ge(semaphore, value)
            if engine.engine == mybir.EngineType.SP:
                engine.sem_inc(sp_passed, 1)

    def steps(engine, body):
        for i in range(FIRST, LOOP_FROM):
            body(i, i % 2)
        with engine.Fori(0, (LOOP_TO - LOOP_FROM) // 2) as n:
            for r in range(2):
                body(n * 2 + (LOOP_FROM + r), r)
        for i in range(LOOP_TO, LAST + 1):
            body(i, i % 2)

    def on(i, d):
        return i.__class__ is not int or valid(i, d)

    sp_passed, pool_passed, _ = passed_by

    with ExitStack() as ctx:
        def sb(name, shape, dt=F32):
            return ctx.enter_context(nc.sbuf_tensor("a_" + name, shape, dt))

        def sem(name):
            return ctx.enter_context(nc.semaphore("a_" + name))

        wq, wk, wv, wo = (sb(n, [P, D]) for n in ("wq", "wk", "wv", "wo"))
        bqk = sb("bqk", [P, 2])
        rows_b = sb("rows_b", [P, 6, D])
        router_b = sb("router_b", [P, 1])
        vg_now = sb("vg_seq", [P, S])
        stats = sb("stats", [P, T, 6])
        mv = sb("mv", [P, T, 2])
        vareps = sb("vareps", [P, T])
        rstd = sb("rstd", [P, T])
        neghalf = sb("neghalf", [P, T])
        z = sb("z", [P, T, D])
        z_t = sb("z_t", [P, S])
        qk = sb("qk", [P, 2, S])
        parts = sb("parts", [P, 3, 2, S], BF16)
        qs = [sb(f"qs{r}", [P, PAIRS, S], BF16) for r in range(2)]
        ks = [sb(f"ks{r}", [P, H, S], BF16) for r in range(2)]
        v_c = [sb(f"v_c{r}", [P, T, D]) for r in range(2)]
        vaug = [sb(f"vaug{r}", [P, T, H, VW]) for r in range(2)]
        mx = sb("mx", [P, 2, H // 2 * T])
        mparts = sb("mparts", [H // 2 * T, 2, SHIFTS, P], BF16)
        mrest = sb("mrest", [H // 2 * T, P])
        minus = sb("minus", [SHIFTS, S], BF16)
        prob = sb("prob", [P, RING, 4, S])
        o_t = sb("o_t", [P, 2, S])
        rden = sb("rden", [P, T, 4])
        attn = sb("attn", [P, T, H, HD])
        a_t = sb("a_t", [P, S])
        r_in = sb("r_in", [P, T, D])
        stats2 = sb("stats2", [P, T, 6])
        mv2 = sb("mv2", [P, T, 2])
        vareps2 = sb("vareps2", [P, T])
        rstd2 = sb("rstd2", [P, T])
        tnorm = sb("tnorm", [P, T, D])
        row = sb("row", [P, T, row_w])
        route = sb("route", [P, 3, T])
        route_i = sb("route_i", [P, 3, T], I32)
        e_iota = sb("e_iota", [P, T, E])
        hot = sb("hot", [P, 2 * T + 1, E])
        number = sb("number", [P, T])
        lower = sb("lower", [P, P])
        place = sb("place", [P, T, E])
        pos_i = sb("pos_i", [P, T], I32)

        stacks = nc.dram_tensor("stacks", (2, 2, H, TERMS, HD, S), BF16, kind="Internal").ap()
        maxima = nc.dram_tensor("maxima", (2, 2, SHIFTS, PAIRS // 2 * T, P), BF16, kind="Internal").ap()

        ps_s = ctx.enter_context(nc.psum_tensor("ps_s", [P, 2, 2, S], F32))
        ps_x = ctx.enter_context(nc.psum_tensor("ps_x", [P, 2, S], F32))
        ps_o = ctx.enter_context(nc.psum_tensor("ps_o", [P, S], F32))
        ps_m = ctx.enter_context(nc.psum_tensor("ps_m", [P, S], F32))

        w_in = sem("w_in")
        consts = sem("consts")
        kconst = sem("kconst")
        misc_full = sem("misc_full")
        misc_free = sem("misc_free")
        vg_copied = sem("vg_copied")
        stat_done = sem("stat_done")
        vareps_done = sem("vareps_done")
        mean_done = sem("mean_done")
        rstd_done = sem("rstd_done")
        z_done = sem("z_done")
        zb_done = sem("zb_done")
        split_step = sem("split_step")
        spilled = sem("spilled")
        qk_done = sem("qk_done")
        middle_done = sem("middle_done")
        mspilled = [sem("mspilled0"), sem("mspilled1")]
        st0_in = sem("st0_in")
        st1_in = sem("st1_in")
        vaug_done = sem("vaug_done")
        mx_mm = sem("mx_mm")
        max_done = sem("max_done")
        msplit_step = sem("msplit_step")
        sh0_in = sem("sh0_in")
        sh1_in = sem("sh1_in")
        qk_mm = sem("qk_mm")
        exp_done = sem("exp_done")
        pv_mm = sem("pv_mm")
        o_done = sem("o_done")
        rden_done = sem("rden_done")
        stat2_done = sem("stat2_done")
        mean2_done = sem("mean2_done")
        vareps2_done = sem("vareps2_done")
        rstd2_done = sem("rstd2_done")
        tnorm_done = sem("tnorm_done")
        x2_step = sem("x2_step")
        x2_done = sem("x2_done")
        kprod_done = sem("kprod_done")
        res_done = sem("res_done")
        keys_done = sem("keys_done")
        route_step = sem("route_step")
        hot_done = sem("hot_done")
        place_step = sem("place_step")
        pos_done = sem("pos_done")
        scattered = sem("scattered")
        block = ctx.enter_context(nc.Block())

        bv, bo, ln_g, ln_b, rw = (rows_b[:, n, :] for n in range(5))
        LOADS = 12
        CONSTS = 14
        STACKS = 3 * 16
        SHIFTED = 16
        SPILLS = 2 * TERMS * 16

        def tokens(b):
            return slice(b * T, b * T + T) if b.__class__ is int else bass.ds(b * T, T)

        def tile_of(b, t):
            return slice(b * T + t, b * T + t + 1) if b.__class__ is int else bass.ds(b * T + t, 1)

        def seq(b):
            return slice(b, b + 1) if b.__class__ is int else bass.ds(b, 1)

        def by_tile(ap):
            return ap.rearrange("p (t d) -> p t d", d=D)

        def bcast_rows(ap):
            return ap.rearrange("p (a d) -> p a d", a=1).broadcast_to([P, T, D])

        @block.sync
        def _(sp):
            for n, w in enumerate((io.Wq, io.Wk, io.Wv, io.Wo)):
                sp.dma_start((wq, wk, wv, wo)[n][:], w).then_inc(w_in, 16)
            sp.dma_start(bqk[:, 0:1], column(io.bq)).then_inc(w_in, 16)
            sp.dma_start(bqk[:, 1:2], column(io.bk)).then_inc(w_in, 16)
            for n, w in enumerate((io.bv, io.bo, io.ln1_g, io.ln1_b)):
                sp.dma_start(rows_b[:, n, :], on_all(w, D)).then_inc(w_in, 16)
            sp.dma_start(rw, io.router_w.rearrange("d a -> a d").broadcast_to([P, D])).then_inc(w_in, 16)
            sp.dma_start(router_b[:], on_all(io.router_b, 1)).then_inc(w_in, 16)
            sp.wait_ge(consts, CONSTS)
            for r in range(2):
                for hh in range(2):
                    own = ks[r][:].rearrange("p (pr hh) t -> p pr hh t", hh=2)
                    sp.dma_start(own[PROWS + SHIFTS * hh:PROWS + SHIFTS * (hh + 1), :, hh, :],
                                 minus[:].rearrange("p (a t) -> p a t", a=1).broadcast_to([SHIFTS, PAIRS, S]))\
                      .then_inc(kconst, 16)

            def spill(b, r):
                for side, order in enumerate((Q_PARTS, K_PARTS)):
                    for n in range(TERMS):
                        sp.dma_start(stacks[r, side, :, n, :, :], parts[:, order[n], side, :]).then_inc(spilled, 16)

            def stack(r, half, landed):
                pairs = slice(half * PAIRS // 2, (half + 1) * PAIRS // 2)
                rows = stacks.rearrange("r s (pr hh) n d t -> r s hh (n d) pr t", hh=2)
                both = stacks.rearrange("r s (pr hh) n d t -> r s (hh n d) pr t", hh=2)
                sp.dma_start(qs[r][0:PROWS, pairs, :], both[r, 0, :, pairs, :]).then_inc(landed, 16)
                for hh in range(2):
                    sp.dma_start(ks[r][:].rearrange("p (pr hh) t -> p pr hh t", hh=2)[HROWS * hh:HROWS * (hh + 1), pairs, hh, :],
                                 rows[r, 1, hh, :, pairs, :]).then_inc(landed, 16)

            def spill_maxima(half):
                own = PAIRS // 2 * T
                for hh in range(2):
                    sp.dma_start(maxima[half, hh].rearrange("n m t -> m n t"), mparts[own * hh:own * (hh + 1), half])\
                      .then_inc(mspilled[half], 16)

            def shift(b, r, half, landed):
                wait(sp, mspilled[half], 32 * (b + 1))
                sp.dma_start(qs[r][PROWS:KROWS, half * PAIRS // 2:(half + 1) * PAIRS // 2, :],
                             maxima[half].rearrange("hh n (pr q) t -> (hh n) pr (q t)", q=T)).then_inc(landed, 16)

            def body(i, r):
                if on(i, 0):
                    wait(sp, msplit_step, 3 * (2 * i + 2))
                    spill_maxima(1)
                if on(i, 1):
                    wait(sp, spilled, SPILLS * (i + 2))
                    wait(sp, qk_mm, i * SLOTS)
                    stack(1 - r, 1, st1_in)
                if on(i, 0):
                    shift(i, r, 1, sh1_in)
                if on(i, 2):
                    wait(sp, split_step, 2 * (i + 3))
                    spill(i + 2, r)
                if on(i, 1):
                    wait(sp, msplit_step, 3 * (2 * i + 3))
                    spill_maxima(0)
                    shift(i + 1, 1 - r, 0, sh0_in)
                if on(i, 2):
                    wait(sp, qk_mm, i * SLOTS + SLOTS // 2)
                    wait(sp, spilled, SPILLS * (i + 3))
                    stack(r, 0, st0_in)

            steps(nc.sync, body)
            sp.wait_ge(st0_in, STACKS * B)
            sp.wait_ge(st1_in, STACKS * B)

        @block.tensor
        def _(pe):
            pe.wait_ge(w_in, 16 * LOADS)
            pe.wait_ge(consts, CONSTS)
            pe.wait_ge(kconst, 64)

            def misc(i, r, name):
                wait(pe, misc_free, uses_before(i, name))
                tiles = [slice(t * P, (t + 1) * P) for t in range(T)]
                if name == "vg":
                    wait(pe, vg_copied, i + 3)
                    for t in tiles:
                        mm = pe.transpose(ps_m[:, t], vg_now[:, t], ident[:])
                elif name == "z":
                    wait(pe, z_done, T * (i + 3))
                    for n, t in enumerate(tiles):
                        mm = pe.transpose(ps_m[:, t], z[:, n, :], ident[:])
                elif name in "qkv":
                    if name == "v":
                        for t in tiles:
                            mm = pe.matmul(ps_m[:, t], z_t[:, t], wv[:], start=True, stop=True)
                    else:
                        mm = pe.matmul(ps_m[:], (wq if name == "q" else wk)[:], z_t[:], start=True, stop=True)
                elif name[:2] == "mx":
                    half = int(name[2])
                    wait(pe, max_done, UNITS * (i + 1) if half else UNITS * (i + 1) + UNITS // 2)
                    mm = pe.transpose(ps_m[0:H // 2 * T, 0:P], mx[:, half, :], ident[:])
                elif name[0] == "o":
                    g = int(name[1])
                    wait(pe, o_done, QUADS * (i - 1) + g + 1 if g == 3 else QUADS * i + g + 1)
                    for t in tiles:
                        mm = pe.transpose(ps_m[:, t], o_t[:, g % 2, t], ident[:])
                elif name == "at":
                    for n, t in enumerate(tiles):
                        mm = pe.transpose(ps_m[:, t], attn[:, n].rearrange("p h d -> p (h d)"), ident[:])
                elif name == "wo":
                    for t in tiles:
                        mm = pe.matmul(ps_m[:, t], a_t[:, t], wo[:], start=True, stop=True)
                elif name == "rk":
                    wait(pe, hot_done, i)
                    ahead = hot[:].rearrange("p t e -> p (t e)")
                    for k in range(T + 1):
                        mm = pe.matmul(ps_m[:, 0:(T + 1) * E], (ones if k else lower)[:],
                                       ahead[:, (T - k) * E:(2 * T + 1 - k) * E], start=(k == 0), stop=(k == T))
                mm.then_inc(misc_full, 1)

            def maxima_of(i, r, n):
                h, qt = n // T, n % T
                wait(pe, max_done, UNITS * (i + 1) + n - 1)
                pe.matmul(ps_x[:, n % 2, :], qs[1 - r][0:PROWS, h // 2, qt * P:(qt + 1) * P],
                          ks[1 - r][0:PROWS, h, :], start=True, stop=True).then_inc(mx_mm, 1)

            def values(b, r, v):
                g, kt = v // T, v % T
                wait(pe, exp_done, b * SLOTS + 2 * v + 2)
                if kt == 0:
                    wait(pe, o_done, QUADS * b + g)
                if v == 0:
                    wait(pe, vaug_done, b + 1)
                for j in range(4):
                    mm = pe.matmul(ps_o[32 * j:32 * j + VW, :], vaug[r][:, kt, 4 * g + j, :], prob[:, v % RING, j, :],
                                   start=(kt == 0), stop=(kt == T - 1))
                mm.then_inc(pv_mm, 1)

            def body(i, r):
                for s in range(SLOTS):
                    for name, at, d in MISC:
                        if at == s and on(i, d):
                            misc(i, r, name)
                    if on(i, 1):
                        if s == 0:
                            wait(pe, st0_in, STACKS * (i + 2))
                        if s == SLOTS // 2:
                            wait(pe, st1_in, STACKS * (i + 2))
                        maxima_of(i, r, 2 * s)
                    if on(i, 0):
                        pair, kt = 2 * (s // 8) + s % 2, (s // 2) % T
                        if s == 0:
                            wait(pe, sh0_in, SHIFTED * (i + 1))
                        if s == SLOTS // 2:
                            wait(pe, sh1_in, SHIFTED * (i + 1))
                        wait(pe, exp_done, i * SLOTS + s - 1)
                        for hh in range(2):
                            mm = pe.matmul(ps_s[:, s % 2, hh, :], ks[r][0:KROWS, 2 * pair + hh, kt * P:(kt + 1) * P],
                                           qs[r][0:KROWS, pair, :], start=True, stop=True)
                        mm.then_inc(qk_mm, 1)
                    if on(i, 1):
                        maxima_of(i, r, 2 * s + 1)
                    if s % 2 == 0:
                        if s < 4 and on(i, -1):
                            values(i - 1, 1 - r, 14 + s // 2)
                        if s >= 4 and on(i, 0):
                            values(i, r, s // 2 - 2)

            steps(nc.tensor, body)

        @block.scalar
        def _(act):
            act.wait_ge(w_in, 16 * LOADS)

            def body(i, r):
                for s in range(SLOTS):
                    if s == slot_of("z") and on(i, 2):
                        act.wait_ge(misc_full, used(i, "z"))
                        act.activation(z_t[:], ps_m[:], ACT.Copy).then_inc(misc_free, 1)
                    if s == slot_of("at") and on(i, -1):
                        act.wait_ge(misc_full, used(i, "at"))
                        act.activation(a_t[:], ps_m[:], ACT.Copy).then_inc(misc_free, 1)
                    for n, name in enumerate("qk"):
                        if s == slot_of(name) and on(i, 2):
                            act.wait_ge(misc_full, used(i, name))
                            if n == 0:
                                wait(act, split_step, 2 * (i + 2))
                            act.activation(qk[:, n, :], ps_m[:], ACT.Identity, bias=bqk[:, n:n + 1]).then_inc(qk_done, 1)
                            if n == 0:
                                wait(act, spilled, SPILLS * (i + 2))
                            act.activation(parts[:, 0, n, :], ps_m[:], ACT.Identity, bias=bqk[:, n:n + 1])\
                               .then_inc(misc_free, 1)
                    if s == MIDDLE and on(i, 2):
                        act.wait_ge(split_step, 2 * (i + 2) + 1)
                        act.activation(parts[:, 1], qk[:], ACT.Identity).then_inc(middle_done, 1)
                    if on(i, 0):
                        act.wait_ge(qk_mm, i * SLOTS + s + 1)
                        if s % 2 == 0:
                            wait(act, pv_mm, i * (SLOTS // 2) + s // 2 + 1 - RING)
                        act.activation(prob[:, (s // 2) % RING, 2 * (s % 2):2 * (s % 2) + 2, :], ps_s[:, s % 2],
                                       ACT.Exp, scale=SCALE).then_inc(exp_done, 1)
                    for g, at, d in ((3, 3, -1), (0, 11, 0), (1, 19, 0), (2, 27, 0)):
                        if s == at and on(i, d):
                            b = i + d
                            act.wait_ge(pv_mm, b * (SLOTS // 2) + 4 * g + 4)
                            wait(act, misc_full, (used(i - 1, "o2"), used(i, "o3"), used(i, "o0"), used(i - 1, "o1"))[g])
                            act.activation(o_t[:, g % 2, :], ps_o[:], ACT.Copy).then_inc(o_done, 1)

            steps(nc.scalar, body)

        @block.gpsimd
        def _(pool):
            pool.memset(neghalf[:], -0.5).then_inc(consts, 1)
            pool.memset(minus[:], -1.0).then_inc(consts, 1)
            pool.memset(hot[:], 0.0).then_inc(consts, 1)
            pool.memset(vaug[0][:], 0.0).then_inc(consts, 1)
            pool.memset(vaug[1][:], 0.0).then_inc(consts, 1)
            pool.memset(lower[:], 1.0).then_inc(consts, 1)
            pool.memset(row[:], 0.0).then_inc(consts, 1)
            pool.iota(e_iota[:], [[0, T], [1, E]], base=0, channel_multiplier=0, allow_small_or_imprecise_dtypes=True)\
                .then_inc(consts, 1)
            pool.iota(count[:], [[SEG, E]], base=0, channel_multiplier=0, allow_small_or_imprecise_dtypes=True)\
                .then_inc(consts, 1)
            pool.iota(number[:], [[P, T]], base=0, channel_multiplier=1, allow_small_or_imprecise_dtypes=True)\
                .then_inc(consts, 1)
            pool.wait_ge(consts, 12)
            pool.affine_select(out=lower[:], in_=lower[:], compare_op=ALU.is_gt, fill=0.0, base=0,
                               pattern=[[1, P]], channel_multiplier=-1).then_inc(consts, 1)
            for r in range(2):
                last = pool.memset(vaug[r][:, :, :, HD:HD + 1], 1.0)
            last.then_inc(consts, 1)
            pool.wait_ge(w_in, 16 * LOADS)

            def passed():
                pool.sem_inc(pool_passed, 1)

            def body(i, r):
                if on(i, 2):
                    wait(pool, misc_full, used(i - 1, "vg"))
                    passed()
                    pool.tensor_copy(vg_now[:].rearrange("p (a s) -> p a s", a=1), vg_t[:, seq(i + 2), :]).then_inc(vg_copied, 1)
                if on(i, 1):
                    wait(pool, misc_free, used(i - 1, "v"))
                    wait(pool, pv_mm, i * (SLOTS // 2))
                    passed()
                    pool.tensor_copy(vaug[1 - r][:, :, :, 0:HD],
                                     v_c[1 - r][:].rearrange("p t (h d) -> p t h d", d=HD)).then_inc(vaug_done, 1)
                if on(i, 2):
                    wait(pool, vareps_done, i + 3)
                    passed()
                    pool.tensor_tensor(rstd[:], vareps[:], neghalf[:], ALU.pow).then_inc(rstd_done, 1)
                    wait(pool, z_done, T * (i + 3))
                    wait(pool, vg_copied, i + 3)
                    passed()
                    pool.tensor_tensor(vg_t[:, seq(i + 2), :].rearrange("p a (t d) -> p (a t) d", d=D), z[:],
                                       bcast_rows(bo), ALU.add).then_inc(zb_done, 1)
                if on(i, -1):
                    wait(pool, vareps2_done, i)
                    passed()
                    pool.tensor_tensor(rstd2[:], vareps2[:], neghalf[:], ALU.pow).then_inc(rstd2_done, 1)
                if on(i, 2):
                    b = i + 2
                    flat = [parts[:, n].rearrange("p s t -> p (s t)") for n in range(3)]
                    left = qk[:].rearrange("p s t -> p (s t)")
                    pool.wait_ge(qk_done, 2 * b + 2)
                    passed()
                    pool.wait_ge(misc_free, used(i, "k"))
                    passed()
                    pool.tensor_tensor(left, left, flat[0], ALU.subtract).then_inc(split_step, 1)
                    pool.wait_ge(middle_done, b + 1)
                    passed()
                    pool.tensor_tensor(flat[2], left, flat[1], ALU.subtract).then_inc(split_step, 1)
                if on(i, -1):
                    wait(pool, tnorm_done, T * i)
                    passed()
                    pool.tensor_tensor(tnorm[:], tnorm[:], bcast_rows(ln_g), ALU.mult).then_inc(x2_step, 1)
                    wait(pool, scattered, 16 * T * (i - 1))
                    pool.wait_ge(x2_step, 2 * i - 1)
                    passed()
                    pool.tensor_tensor(row[:, :, 0:D], tnorm[:], bcast_rows(ln_b), ALU.add).then_inc(x2_step, 1)
                    pool.tensor_copy(row[:, :, D:2 * D], x_tok[:, tokens(i - 1), :]).then_inc(res_done, 1)
                    pool.tensor_copy(row[:, :, 2 * D], number[:]).then_inc(res_done, 1)
                    pool.wait_ge(res_done, 2 * i)
                    passed()
                    pool.tensor_scalar(number[:], number[:], float(S), 0.0, ALU.add, ALU.add).then_inc(x2_done, 1)
                    pool.wait_ge(x2_step, 2 * i)
                    passed()
                    pool.tensor_tensor(tnorm[:], row[:, :, 0:D], bcast_rows(rw), ALU.mult).then_inc(kprod_done, 1)
                if on(i, -1):
                    pool.wait_ge(pos_done, i)
                    pool.wait_ge(x2_done, i)
                    passed()
                    for t in range(T):
                        pool.indirect_dma_start(rows_dram, bass.IndirectOffsetOnAxis(ap=pos_i[:, t:t + 1], axis=0),
                                                row[:, t, :], None).then_inc(scattered, 16)

            steps(nc.gpsimd, body)
            pool.wait_ge(scattered, 16 * T * B)

        @block.vector
        def _(dve):
            for r in range(2):
                dve.memset(ks[r][:].rearrange("p h t -> p (h t)").bitcast(F32), 0.0).then_inc(consts, 1)
            dve.wait_ge(w_in, 16 * LOADS)
            dve.wait_ge(consts, CONSTS)

            def split_maxima(b, half, r, use):
                n = 2 * b + half
                rows = slice(0, H // 2 * T)
                dve.wait_ge(misc_full, use)
                wait(dve, (sh0_in, sh1_in)[half], SHIFTED * b)
                dve.tensor_copy(mparts[:, half, 0, :], ps_m[rows, 0:P]).then_inc(msplit_step, 1)
                dve.wait_ge(msplit_step, 3 * n + 1)
                dve.tensor_tensor(mrest[:], ps_m[rows, 0:P], mparts[:, half, 0, :], ALU.subtract).then_inc(misc_free, 1)
                dve.wait_ge(misc_free, use)
                dve.tensor_copy(mparts[:, half, 1, :], mrest[:]).then_inc(msplit_step, 1)
                dve.wait_ge(msplit_step, 3 * n + 2)
                dve.tensor_tensor(mparts[:, half, 2, :], mrest[:], mparts[:, half, 1, :], ALU.subtract)\
                   .then_inc(msplit_step, 1)

            def normalise_quad(b, g, use):
                dve.wait_ge(misc_full, use)
                sums = ps_m[:].rearrange("p (t j c) -> p t j c", t=T, c=VW)
                dve.reciprocal(rden[:].rearrange("p t (j a) -> p t j a", a=1), sums[:, :, :, HD:HD + 1]).then_inc(rden_done, 1)
                dve.wait_ge(rden_done, QUADS * b + g + 1)
                dve.tensor_tensor(attn[:, :, 4 * g:4 * g + 4, :], sums[:, :, :, 0:HD],
                                  rden[:].rearrange("p t (j a) -> p t j a", a=1).broadcast_to([P, T, 4, HD]),
                                  ALU.mult).then_inc(misc_free, 1)

            def body(i, r):
                for s in range(SLOTS):
                    if s == 1 and on(i, 0):
                        split_maxima(i, 1, r, used(i, "mx1"))
                    if s == 3 and on(i, 2):
                        dve.wait_ge(misc_full, used(i, "vg"))
                        dve.tensor_tensor(x_tok[:, tokens(i + 2), :], x_tok[:, tokens(i + 2), :], by_tile(ps_m[:]), ALU.add)\
                           .then_inc(misc_free, 1)
                    if s == 4 and on(i, 2):
                        for t in range(T):
                            dve.bn_stats(stats[:, t, :], x_tok[:, tile_of(i + 2, t), :]).then_inc(stat_done, 1)
                    if s == 5 and on(i, 2):
                        for t in range(T):
                            dve.bn_aggr(mv[:, t, :], stats[:, t, :]).then_inc(mean_done, 1)
                        dve.wait_ge(mean_done, T * (i + 3))
                        dve.tensor_scalar(vareps[:], mv[:, :, 1], EPS, None, ALU.add).then_inc(vareps_done, 1)
                    if s == 5 and on(i, -1):
                        normalise_quad(i - 1, 3, used(i, "o3"))
                    if s == 7 and on(i, 2):
                        dve.wait_ge(rstd_done, i + 3)
                        wait(dve, misc_full, used(i - 1, "z"))
                        wait(dve, zb_done, i + 2)
                        for t in range(T):
                            dve.tensor_scalar(z[:, t:t + 1, :], x_tok[:, tile_of(i + 2, t), :], mv[:, t, 0:1], rstd[:, t:t + 1],
                                              ALU.subtract, ALU.mult).then_inc(z_done, 1)
                    if s == 10 and on(i, -1):
                        dve.wait_ge(misc_full, used(i, "wo"))
                        wait(dve, tnorm_done, T * (i - 1))
                        dve.tensor_tensor(r_in[:], vg_t[:, seq(i - 1), :].rearrange("p a (t d) -> p (a t) d", d=D),
                                          by_tile(ps_m[:]), ALU.add).then_inc(misc_free, 1)
                    if s == 11 and on(i, -1):
                        dve.wait_ge(misc_free, used(i, "wo"))
                        wait(dve, mean2_done, T * (i - 1))
                        for t in range(T):
                            dve.bn_stats(stats2[:, t, :], r_in[:, t, :]).then_inc(stat2_done, 1)
                    if s == 12 and on(i, -1):
                        for t in range(T):
                            dve.bn_aggr(mv2[:, t, :], stats2[:, t, :]).then_inc(mean2_done, 1)
                        dve.wait_ge(mean2_done, T * i)
                        dve.tensor_scalar(vareps2[:], mv2[:, :, 1], EPS, None, ALU.add).then_inc(vareps2_done, 1)
                    if s == 14 and on(i, 0):
                        normalise_quad(i, 0, used(i, "o0"))
                    if s == 16 and on(i, 2):
                        dve.wait_ge(misc_full, used(i, "v"))
                        wait(dve, vaug_done, i + 1)
                        dve.tensor_tensor(v_c[r][:], by_tile(ps_m[:]), bcast_rows(bv), ALU.add).then_inc(misc_free, 1)
                    if s == 14 and on(i, -1):
                        dve.wait_ge(rstd2_done, i)
                        wait(dve, keys_done, i - 1)
                        for t in range(T):
                            dve.tensor_scalar(tnorm[:, t, :], r_in[:, t, :], mv2[:, t, 0:1], rstd2[:, t:t + 1],
                                              ALU.subtract, ALU.mult).then_inc(tnorm_done, 1)
                    if s == 18 and on(i, 1):
                        split_maxima(i + 1, 0, 1 - r, used(i, "mx0"))
                    if s == 21 and on(i, 0):
                        normalise_quad(i, 1, used(i, "o1"))
                    if s == 22 and on(i, -1):
                        n = 5 * (i - 1)
                        dve.wait_ge(kprod_done, i)
                        dve.tensor_reduce(route[:, 0, :], tnorm[:], AX.X, ALU.add).then_inc(route_step, 1)
                        dve.wait_ge(route_step, n + 1)
                        dve.tensor_scalar(route[:, 1, :], route[:, 0, :], router_b[:, 0:1], None, ALU.add)\
                           .then_inc(route_step, 1)
                        dve.wait_ge(route_step, n + 2)
                        dve.tensor_copy(route_i[:, 0, :], route[:, 1, :]).then_inc(route_step, 1)
                        dve.wait_ge(route_step, n + 3)
                        dve.tensor_tensor(route[:, 2, :], route_i[:, 0, :], route[:, 1, :], ALU.is_gt).then_inc(route_step, 1)
                        dve.wait_ge(route_step, n + 4)
                        dve.tensor_tensor(route_i[:, 1, :], route_i[:, 0, :], route[:, 2, :], ALU.subtract)\
                           .then_inc(route_step, 1)
                    if s == 23 and on(i, -1):
                        dve.wait_ge(route_step, 5 * i)
                        dve.tensor_scalar(route_i[:, 2, :], route_i[:, 1, :], E - 1, None, ALU.bitwise_and)\
                           .then_inc(keys_done, 1)
                        dve.wait_ge(keys_done, i)
                        dve.tensor_tensor(hot[:, T:2 * T, :], route_i[:, 2, :].rearrange("p (t a) -> p t a", a=1)
                                          .broadcast_to([P, T, E]), e_iota[:], ALU.is_equal).then_inc(hot_done, 1)
                    if s == 26 and on(i, -1):
                        ranks = ps_m[:, 0:(T + 1) * E].rearrange("p (t e) -> p t e", e=E)
                        dve.wait_ge(misc_full, used(i, "rk"))
                        wait(dve, scattered, 16 * T * (i - 1))
                        dve.tensor_tensor(place[:], ranks[:, 0:T, :], count[:].rearrange("p (a e) -> p a e", a=1)
                                          .broadcast_to([P, T, E]), ALU.add).then_inc(place_step, 1)
                        dve.wait_ge(place_step, 3 * i - 2)
                        dve.tensor_tensor(count[:], count[:], ranks[:, T, :], ALU.add).then_inc(misc_free, 1)
                        dve.wait_ge(misc_free, used(i, "rk"))
                        dve.tensor_tensor(place[:], place[:], hot[:, T:2 * T, :], ALU.mult).then_inc(place_step, 1)
                        dve.wait_ge(place_step, 3 * i - 1)
                        dve.tensor_reduce(route[:, 0, :], place[:], AX.X, ALU.add).then_inc(place_step, 1)
                        dve.wait_ge(place_step, 3 * i)
                        dve.tensor_copy(pos_i[:], route[:, 0, :]).then_inc(pos_done, 1)
                    if s == 29 and on(i, 0):
                        normalise_quad(i, 2, used(i, "o2"))
                    if s == 3 and on(i, 2):
                        dve.wait_ge(misc_free, used(i, "vg"))
                        wait(dve, mean_done, T * (i + 2))
                    if s == 4 and on(i, 2):
                        dve.wait_ge(stat_done, T * (i + 3))
                        wait(dve, z_done, T * (i + 2))
                    if s == 11 and on(i, -1):
                        dve.wait_ge(stat2_done, T * i)
                        wait(dve, tnorm_done, T * (i - 1))
                    if on(i, 1):
                        for n in (2 * s, 2 * s + 1):
                            h, qt = n // T, n % T
                            half = h // (H // 2)
                            col = (h % 2 * (PAIRS // 2) + h // 2 % (PAIRS // 2)) * T + qt
                            if n == 0:
                                wait(dve, misc_full, used(i - 1, "mx0"))
                            if n == UNITS // 2:
                                wait(dve, misc_full, used(i, "mx1"))
                            dve.wait_ge(mx_mm, UNITS * (i + 1) + n + 1)
                            dve.tensor_reduce(mx[:, half, col:col + 1], ps_x[:, n % 2, :], AX.X, ALU.max)\
                               .then_inc(max_done, 1)

            steps(nc.vector, body)


def experts_program(nc, io, ident, rows_dram, seg, row_w, block_w, count, passed_by, out):
    B, S, D = io.x.shape
    E, _, F = io.W1.shape
    N = B * S
    NB = N // block_w + E - 1
    T = block_w // P
    FT = F // P
    RING = 3
    LOOPS = (NB - RING - 1) // RING
    assert NB == RING * (LOOPS + 1) + 1

    sp_passed, pool_passed, dve_passed = passed_by

    with ExitStack() as ctx:
        def sb(name, shape, dt=F32):
            return ctx.enter_context(nc.sbuf_tensor("e_" + name, shape, dt))

        def sem(name):
            return ctx.enter_context(nc.semaphore("e_" + name))

        padding = sb("padding", [P, T, row_w])
        numbers = sb("numbers", [P, T])
        seg_start = sb("seg_start", [P, E])
        block_no = sb("block_no", [P, NB])
        filled = sb("filled", [P, E])
        blocks_i = sb("blocks_i", [P, 3, E], I32)
        count_i = sb("count_i", [P, E], I32)
        n_blocks = sb("n_blocks", [P, E])
        ends = sb("ends", [P, E])
        passed_e = sb("passed_e", [P, NB, E])
        expert = sb("expert", [P, NB])
        first = sb("first", [P, NB])
        table = sb("table", [P, 2, NB], I32)
        work = sb("work", [P, 3, NB])
        neghalf = sb("neghalf", [P, T])
        ln_gb = sb("ln_gb", [P, 2, D])
        rows = [sb(f"rows{r}", [P, T, row_w]) for r in range(RING)]
        w1 = [sb(f"w1{r}", [P, F]) for r in range(RING)]
        w2 = [sb(f"w2{r}", [P, FT, D]) for r in range(RING)]
        biases_all = sb("biases_all", [P, E, FT + 1])
        biases = [sb(f"biases{r}", [P, 1, FT + 1]) for r in range(RING)]
        x_t = [sb(f"x_t{r}", [P, block_w]) for r in range(RING)]
        hid = [sb(f"hid{r}", [P, FT, block_w]) for r in range(RING)]
        y_t = [sb(f"y_t{r}", [P, block_w]) for r in range(RING)]
        r_in = sb("r_in", [P, T, D])
        stats = sb("stats", [P, T, 6])
        mv = sb("mv", [P, T, 2])
        vareps = sb("vareps", [P, T])
        rstd = sb("rstd", [P, T])
        tn = sb("tn", [P, T, D])
        ids = [sb(f"ids{r}", [P, T], I32) for r in range(RING)]
        result = [sb(f"result{r}", [P, T, D]) for r in range(RING)]
        ps_a = ctx.enter_context(nc.psum_tensor("ps_a", [P, block_w], F32))
        ps_f = ctx.enter_context(nc.psum_tensor("ps_f", [P, FT, block_w], F32))
        ps_y = ctx.enter_context(nc.psum_tensor("ps_y", [P, block_w], F32))
        ps_b = ctx.enter_context(nc.psum_tensor("ps_b", [P, block_w], F32))

        consts = sem("consts")
        params_in = sem("params_in")
        step = sem("step")
        table_done = sem("table_done")
        padded = sem("padded")
        rows_in = [sem(f"rows_in{r}") for r in range(RING)]
        weights_in = [sem(f"weights_in{r}") for r in range(RING)]
        xt_mm = sem("xt_mm")
        xt_done = sem("xt_done")
        hid_mm = sem("hid_mm")
        hid_done = sem("hid_done")
        y_mm = sem("y_mm")
        y_done = sem("y_done")
        back_mm = sem("back_mm")
        r_done = sem("r_done")
        stat_done = sem("stat_done")
        mean_done = sem("mean_done")
        vareps_done = sem("vareps_done")
        rstd_done = sem("rstd_done")
        tn_done = sem("tn_done")
        affine = sem("affine")
        result_done = sem("result_done")
        ids_done = sem("ids_done")
        sent = [sem(f"sent{r}") for r in range(RING)]
        block = ctx.enter_context(nc.Block())

        def wait(engine, semaphore, value):
            if value.__class__ is not int or value > 0:
                engine.wait_ge(semaphore, value)

        def blocks(engine, body):
            for j in range(RING):
                body(j, j, 0)
            with engine.Fori(0, LOOPS) as n:
                for r in range(RING):
                    body(n * RING + (RING + r), r, n + 1)
            body(NB - 1, 0, LOOPS + 1)

        def bcast(ap):
            return ap.rearrange("p (a d) -> p a d", a=1).broadcast_to([P, T, D])

        @block.gpsimd
        def _(pool):
            pool.memset(padding[:], 0.0).then_inc(consts, 1)
            pool.memset(neghalf[:], -0.5).then_inc(consts, 1)
            pool.iota(numbers[:], [[1, T]], base=N, channel_multiplier=T, allow_small_or_imprecise_dtypes=True).then_inc(consts, 1)
            pool.iota(seg_start[:], [[seg, E]], base=0, channel_multiplier=0, allow_small_or_imprecise_dtypes=True)\
                .then_inc(consts, 1)
            pool.iota(block_no[:], [[1, NB]], base=0, channel_multiplier=0, allow_small_or_imprecise_dtypes=True)\
                .then_inc(consts, 1)
            pool.wait_ge(consts, 5)
            pool.tensor_copy(padding[:, :, 2 * D], numbers[:]).then_inc(consts, 1)

            def body(j, r, before):
                pool.wait_ge(vareps_done, j + 1)
                pool.tensor_tensor(rstd[:], vareps[:], neghalf[:], ALU.pow).then_inc(rstd_done, 1)
                pool.wait_ge(result_done, j + 1)
                pool.wait_ge(ids_done, j + 1)
                pool.sem_inc(pool_passed, 1)
                for t in range(T):
                    pool.indirect_dma_start(out.rearrange("b s d -> (b s) d"),
                                            bass.IndirectOffsetOnAxis(ap=ids[r][:, t:t + 1], axis=0),
                                            result[r][:, t, :], None, bounds_check=N - 1, oob_is_err=False).then_inc(sent[r], 16)

            blocks(nc.gpsimd, body)
            for r in range(RING):
                pool.wait_ge(sent[r], 16 * T * ((NB - 1 - r) // RING + 1))

        @block.sync
        def _(sp):
            sp.dma_start(ln_gb[:, 0, :], on_all(io.ln2_g, D)).then_inc(params_in, 16)
            sp.dma_start(ln_gb[:, 1, :], on_all(io.ln2_b, D)).then_inc(params_in, 16)
            for e in range(E):
                sp.dma_start(biases_all[:, e, 0:FT], io.b1[e].rearrange("(f p) -> p f", p=P),
                             allow_slow_non_contiguous=True).then_inc(params_in, 16)
                sp.dma_start(biases_all[:, e, FT:FT + 1], column(io.b2[e])).then_inc(params_in, 16)
            sp.wait_ge(params_in, 32 * (E + 1))
            sp.wait_ge(consts, 6)
            for k in range(E - 1):
                sp.dma_start(rows_dram[E * seg + k * block_w:E * seg + (k + 1) * block_w, :]
                             .rearrange("(p t) w -> p t w", t=T), padding[:]).then_inc(padded, 16)
            sp.wait_ge(table_done, 1)
            for e in range(E):
                end = sp.value_load(count_i[0:1, e:e + 1], min_val=e * seg, max_val=e * seg + N)
                sp.dma_start(rows_dram[bass.ds(end, block_w), :].rearrange("(p t) w -> p t w", t=T), padding[:])\
                  .then_inc(padded, 16)
            sp.wait_ge(padded, 16 * (2 * E - 1))

            def body(j, r, before):
                at = slice(j, j + 1) if j.__class__ is int else bass.ds(j, 1)
                wait(sp, result_done, j + (1 - RING))
                sp.sem_inc(sp_passed, 1)
                wait(sp, y_done, j + (1 - RING))
                sp.sem_inc(sp_passed, 1)
                start = sp.value_load(table[0:1, 1, at], min_val=0, max_val=E * seg + (E - 2) * block_w)
                sp.dma_start(rows[r][:], rows_dram[bass.ds(start, block_w), :].rearrange("(t p) w -> p t w", p=P))\
                  .then_inc(rows_in[r], 16)
                e = sp.value_load(table[0:1, 0, at], min_val=0, max_val=E - 1)
                one = bass.ds(e, 1)
                sp.dma_start(w1[r][:], io.W1[one].rearrange("a p f -> p (a f)")).then_inc(weights_in[r], 16)
                sp.dma_start(w2[r][:], io.W2[one].rearrange("a (f p) d -> p (a f) d", p=P)).then_inc(weights_in[r], 16)
                sp.dma_start(biases[r][:], biases_all[:, one, :]).then_inc(weights_in[r], 16)

            blocks(nc.sync, body)

        @block.tensor
        def _(pe):
            def turn(j, r, arrived):
                pe.wait_ge(rows_in[r], 16 * arrived)
                wait(pe, xt_done, j)
                for t in range(T):
                    mm = pe.transpose(ps_a[:, t * P:(t + 1) * P], rows[r][:, t, 0:D], ident[:])
                mm.then_inc(xt_mm, 1)

            def layer1(j, r, arrived):
                pe.wait_ge(weights_in[r], 48 * arrived)
                pe.wait_ge(xt_done, j + 1)
                for f in range(FT):
                    wait(pe, hid_done, (j - 1) * FT + f + 1)
                    pe.matmul(ps_f[:, f, :], w1[r][:, f * P:(f + 1) * P], x_t[r][:], start=True, stop=True).then_inc(hid_mm, 1)

            def layer2(j, r, before):
                wait(pe, y_done, j)
                for f in range(FT):
                    if f == FT // 2 and (j.__class__ is not int or j < NB - 1):
                        turn(j + 1, (r + 1) % RING, before + 1 + (r == RING - 1))
                    pe.wait_ge(hid_done, j * FT + f + 1)
                    mm = pe.matmul(ps_y[:], w2[r][:, f, :], hid[r][:, f, :], start=(f == 0), stop=(f == FT - 1))
                mm.then_inc(y_mm, 1)

            def back(j, r):
                pe.wait_ge(y_done, j + 1)
                wait(pe, r_done, j)
                for t in range(T):
                    mm = pe.transpose(ps_b[:, t * P:(t + 1) * P], y_t[r][:, t * P:(t + 1) * P], ident[:])
                mm.then_inc(back_mm, 1)

            def body(j, r, before):
                layer1(j, r, before + 1)
                if j.__class__ is not int or j > 0:
                    back(j - 1, (r - 1) % RING)
                layer2(j, r, before)

            turn(0, 0, 1)
            blocks(nc.tensor, body)
            back(NB - 1, 0)

        @block.scalar
        def _(act):
            def inputs(j, r):
                act.wait_ge(xt_mm, j + 1)
                wait(act, hid_mm, (j - 1) * FT)
                act.activation(x_t[r][:], ps_a[:], ACT.Copy).then_inc(xt_done, 1)

            def middle(j, r):
                for f in range(FT):
                    act.wait_ge(hid_mm, j * FT + f + 1)
                    if f == 0:
                        wait(act, y_mm, j - 1)
                    act.activation(hid[r][:, f, :], ps_f[:, f, :], ACT.Relu, bias=biases[r][:, 0, f:f + 1]).then_inc(hid_done, 1)

            def end(j, r):
                act.wait_ge(y_mm, j + 1)
                wait(act, back_mm, j - 1)
                act.activation(y_t[r][:], ps_y[:], ACT.Identity, bias=biases[r][:, 0, FT:FT + 1]).then_inc(y_done, 1)

            def body(j, r, before):
                act.wait_ge(weights_in[r], 48 * (before + 1))
                middle(j, r)
                if j.__class__ is not int or j < NB - 1:
                    inputs(j + 1, (r + 1) % RING)
                end(j, r)

            inputs(0, 0)
            blocks(nc.scalar, body)

        @block.vector
        def _(dve):
            def chain(ins):
                ins.then_inc(step, 1)
                chain.n += 1
                dve.wait_ge(step, chain.n)
            chain.n = 0
            dve.wait_ge(consts, 6)
            dve.tensor_copy(count_i[:], count[:]).then_inc(consts, 1)
            chain(dve.tensor_tensor(filled[:], count[:], seg_start[:], ALU.subtract))
            chain(dve.tensor_scalar(blocks_i[:, 0, :], filled[:], float(block_w - 1), None, ALU.add))
            chain(dve.tensor_scalar(blocks_i[:, 1, :], blocks_i[:, 0, :], -block_w, None, ALU.bitwise_and))
            chain(dve.tensor_scalar(n_blocks[:], blocks_i[:, 1, :], 1.0 / block_w, None, ALU.mult))
            chain(dve.tensor_copy(ends[:, 0:1], n_blocks[:, 0:1]))
            for e in range(1, E):
                chain(dve.tensor_tensor(ends[:, e:e + 1], ends[:, e - 1:e], n_blocks[:, e:e + 1], ALU.add))
            chain(dve.tensor_tensor(passed_e[:], block_no[:].rearrange("p (n a) -> p n a", a=1).broadcast_to([P, NB, E]),
                                    ends[:].rearrange("p (a e) -> p a e", a=1).broadcast_to([P, NB, E]), ALU.is_ge))
            chain(dve.tensor_reduce(expert[:], passed_e[:], AX.X, ALU.add))
            chain(dve.tensor_tensor(passed_e[:], passed_e[:], n_blocks[:].rearrange("p (a e) -> p a e", a=1)
                                    .broadcast_to([P, NB, E]), ALU.mult))
            chain(dve.tensor_reduce(first[:], passed_e[:], AX.X, ALU.add))
            chain(dve.tensor_tensor(work[:, 0, :], block_no[:], first[:], ALU.subtract))
            chain(dve.tensor_scalar(work[:, 1, :], work[:, 0, :], float(block_w), None, ALU.mult))
            chain(dve.tensor_scalar(work[:, 2, :], expert[:], float(seg), None, ALU.mult))
            chain(dve.tensor_tensor(table[:, 1, :], work[:, 1, :], work[:, 2, :], ALU.add))
            dve.wait_ge(consts, 7)
            dve.tensor_scalar(table[:, 0, :], expert[:], float(E - 1), None, ALU.min).then_inc(table_done, 1)
            dve.wait_ge(params_in, 32 * (E + 1))

            def passed():
                dve.sem_inc(dve_passed, 1)

            def body(j, r, before):
                dve.wait_ge(back_mm, j + 1)
                wait(dve, sent[r], before * (16 * T))
                passed()
                dve.tensor_copy(ids[r][:], rows[r][:, :, 2 * D]).then_inc(ids_done, 1)
                wait(dve, tn_done, T * j)
                dve.tensor_tensor(r_in[:], rows[r][:, :, 0:D], ps_b[:].rearrange("p (t d) -> p t d", d=D), ALU.add)\
                   .then_inc(r_done, 1)
                dve.wait_ge(r_done, j + 1)
                for t in range(T):
                    dve.bn_stats(stats[:, t, :], r_in[:, t, :]).then_inc(stat_done, 1)
                dve.wait_ge(stat_done, T * (j + 1))
                passed()
                for t in range(T):
                    dve.bn_aggr(mv[:, t, :], stats[:, t, :]).then_inc(mean_done, 1)
                dve.wait_ge(mean_done, T * (j + 1))
                dve.tensor_scalar(vareps[:], mv[:, :, 1], EPS, None, ALU.add).then_inc(vareps_done, 1)
                dve.wait_ge(rstd_done, j + 1)
                wait(dve, result_done, j)
                for t in range(T):
                    dve.tensor_scalar(tn[:, t, :], r_in[:, t, :], mv[:, t, 0:1], rstd[:, t:t + 1],
                                      ALU.subtract, ALU.mult).then_inc(tn_done, 1)
                dve.wait_ge(tn_done, T * (j + 1))
                dve.tensor_tensor(tn[:], tn[:], bcast(ln_gb[:, 0, :]), ALU.mult).then_inc(affine, 1)
                dve.wait_ge(affine, 2 * j + 1)
                dve.tensor_tensor(tn[:], tn[:], bcast(ln_gb[:, 1, :]), ALU.add).then_inc(affine, 1)
                dve.wait_ge(affine, 2 * j + 2)
                dve.tensor_tensor(result[r][:], tn[:], rows[r][:, :, D:2 * D], ALU.add).then_inc(result_done, 1)

            blocks(nc.vector, body)


def program(nc, io, out):
    B, S, D = io.x.shape
    E = io.W1.shape[0]
    TILES = B * S // P
    BLOCK_W = 512
    ROW_W = 2 * D + 4
    SEG = B * S + BLOCK_W
    with ExitStack() as ctx:
        ident = ctx.enter_context(nc.sbuf_tensor("ident", [P, P], F32))
        ones = ctx.enter_context(nc.sbuf_tensor("ones", [P, P], F32))
        count = ctx.enter_context(nc.sbuf_tensor("count", [P, E], F32))
        passed_by = [ctx.enter_context(nc.semaphore(f"{engine}_passed")) for engine in ("sp", "pool", "dve")]
        rows_dram = nc.dram_tensor("rows", (E * SEG + (E - 1) * BLOCK_W, ROW_W), F32, kind="Internal").ap()
        with ExitStack() as tokens:
            x_tok = tokens.enter_context(nc.sbuf_tensor("x_tok", [P, TILES, D], F32))
            vg_t = tokens.enter_context(nc.sbuf_tensor("vg_t", [P, B, S], F32))
            memory_program(nc, io, x_tok, vg_t, ident, ones)
            attention_program(nc, io, x_tok, vg_t, ident, ones, rows_dram, SEG, ROW_W, count, passed_by)
        experts_program(nc, io, ident, rows_dram, SEG, ROW_W, BLOCK_W, count, passed_by, out)


def kernel(**inputs):
    import numpy as np
    import concourse.bacc as bacc
    from concourse.bass_utils import run_bass_kernel_spmd

    nc = bacc.Bacc("TRN2", target_bir_lowering=False, num_devices=1)
    arrays, aps = {}, []
    for name in ["L0_attn_" + n for n in _ATTN] + ["L0_ffn_" + n for n in _FFN]:
        a = np.ascontiguousarray(inputs[name])
        arrays[f"in_{name}"] = a
        aps.append(nc.dram_tensor(f"in_{name}", a.shape, mybir.dt.from_np(a.dtype), kind="ExternalInput").ap())
    out = nc.dram_tensor("out_0", inputs["L0_attn_x"].shape, F32, kind="ExternalOutput").ap()
    program(nc, Inputs(*aps), out)
    return run_bass_kernel_spmd(nc, [arrays], core_ids=[0]).results[0]["out_0"]
```

```python
from collections import namedtuple
from contextlib import ExitStack

import concourse.bass as bass
from concourse import mybir

F32 = mybir.dt.float32
BF16 = mybir.dt.bfloat16
I32 = mybir.dt.int32
ACT = mybir.ActivationFunctionType
ALU = mybir.AluOpType
AX = mybir.AxisListType

P = 128
EPS = 1e-5
N_HEAD = 16
SPLIT = 3
PRODUCTS = 6
VALUE_W = 32


_ATTN = ("x", "M_init", "eta_w", "eta_b", "alpha_w", "alpha_b", "gate_w", "gate_b", "vg_w1", "vg_w2")
_FFN = ("Wq", "bq", "Wk", "bk", "Wv", "bv", "Wo", "bo", "router_w", "router_b", "W1", "b1", "W2", "b2",
        "ln1_g", "ln1_b", "ln2_g", "ln2_b")
Inputs = namedtuple("Inputs", _ATTN + _FFN)


def column(ap):
    return ap.rearrange("(p a) -> p a", a=1)


def on_all(ap, n):
    return ap.rearrange("(a n) -> a n", a=1).broadcast_to([P, n])


def memory_program(nc, io, x_tok, vg_t, ident, ones, later_loads, later_constants):
    B, S, D = io.x.shape
    TILES = B * S // P
    CH = 64
    NCH = S // CH
    HALVES = P // CH
    TPB = S // P
    CW = CH + 1
    G = 2
    GB = B // G
    QUARTERS = 4
    STRIP = 32
    STRIPS = P // STRIP
    TQ = TILES // QUARTERS

    with ExitStack() as ctx:
        def sb(name, shape, dt=F32):
            return ctx.enter_context(nc.sbuf_tensor(name, shape, dt))

        def sem(name):
            return ctx.enter_context(nc.semaphore(name))

        xhat = sb("xhat", [P, B, NCH, CW])
        key = sb("key", [P, B, NCH])
        mt = sb("mt", [P, B, D])
        coef_keep = sb("coef_keep", [P, NCH, B])
        coef_err = sb("coef_err", [P, NCH, B])
        w1t = sb("w1t", [P, D])
        w2t = sb("w2t", [P, D])
        minit_t = sb("minit_t", [P, D])

        with ExitStack() as c2:
            def sb2(name, shape, dt=F32):
                return c2.enter_context(nc.sbuf_tensor(name, shape, dt))

            def sem2(name):
                return c2.enter_context(nc.semaphore(name))

            xn = vg_t[:].rearrange("p b (j d) -> p (b j) d", d=D)
            stats = sb2("stats", [P, TILES, 6])
            meanvar = sb2("meanvar", [P, TILES, 2])
            vareps = sb2("vareps", [P, TILES])
            rstd = sb2("rstd", [P, TILES])
            neghalf = sb2("neghalf", [P, TILES])
            sumsq = sb2("sumsq", [P, 3, TILES])
            kinv = sb2("kinv", [P, TILES])
            halfmask = sb2("halfmask", [P, HALVES])
            key_w = sb2("key_w", [P, TILES, 2, HALVES])
            vecs = sb2("vecs", [P, 3])
            gate_rep = sb2("gate_rep", [P, P])
            token_rep = sb2("token_rep", [P, 2, STRIP])
            strips = sb2("strips", [P, STRIPS])
            select = sb2("select", [P, STRIPS, P])
            strip_bias = sb2("strip_bias", [P, 1])
            sig_sum = sb2("sig_sum", [P, B // 2, NCH])
            biases = sb2("biases", [P, 3])
            raw_w = sb2("raw_w", [P, 3, D])
            sig = sb2("sig", [P, B // 2, S])
            gate = sb2("gate", [P, B, NCH])
            alpha = sb2("alpha", [P, B, NCH])
            eta = sb2("eta", [P, B, NCH])
            ps_t = c2.enter_context(nc.psum_tensor("ps_t", [P, 2, S], F32))
            ps_g = c2.enter_context(nc.psum_tensor("ps_g", [P, 2, S], F32))
            ps_k = c2.enter_context(nc.psum_tensor("ps_k", [P, TILES, 2, HALVES], F32))
            ps_w = c2.enter_context(nc.psum_tensor("ps_w", [P, 4, P], F32))
            ps_b = c2.enter_context(nc.psum_tensor("ps_means", [P, STRIPS, B // 2, NCH], F32))

            x_in = [sem2(f"x_in{q}") for q in range(QUARTERS)]
            w_in = sem2("w_in")
            consts = sem2("consts")
            stat_done = sem2("stat_done")
            mean_done = sem2("mean_done")
            vareps_done = sem2("vareps_done")
            rstd_done = sem2("rstd_done")
            xn_done = sem2("xn_done")
            sumsq_step = sem2("sumsq_step")
            kinv_done = sem2("kinv_done")
            key_w_done = sem2("key_w_done")
            t_done = sem2("t_done")
            xhat_done = sem2("xhat_done")
            wt_done = sem2("wt_done")
            wt_copied = sem2("wt_copied")
            rep_done = sem2("rep_done")
            gates_mm = sem2("gates_mm")
            bias_done = sem2("bias_done")
            sum_done = sem2("sum_done")
            sig_done = sem2("sig_done")
            means_mm = sem2("means_mm")
            key_mm = sem2("key_mm")
            key_done = sem2("key_done")
            gate_mm = sem2("gate_mm")
            gate_done = sem2("gate_done")
            coef_step = sem2("coef_step")

            block = c2.enter_context(nc.Block())
            x_rows = io.x.rearrange("b s d -> (b s) d").rearrange("(i p) d -> p i d", p=P)

            REPS = 3 + STRIPS

            def quarter(q):
                return slice(q * TQ, (q + 1) * TQ)

            @block.sync
            def _(sp):
                for q in range(QUARTERS):
                    sp.dma_start(x_tok[:, quarter(q), :], x_rows[:, quarter(q), :]).then_inc(x_in[q], 16)
                later_loads(sp)

            @block.scalar
            def _(act):
                for n, w in enumerate((io.M_init, io.vg_w1, io.vg_w2)):
                    act.dma_start(raw_w[:, n, :], w).then_inc(w_in, 16)
                for n, (w, b) in enumerate(((io.eta_w, io.eta_b), (io.alpha_w, io.alpha_b), (io.gate_w, io.gate_b))):
                    act.dma_start(vecs[:, n:n + 1], column(w)).then_inc(w_in, 16)
                    act.dma_start(biases[:, n:n + 1], on_all(b, 1)).then_inc(w_in, 16)
                act.wait_ge(w_in, 16 * 9)
                for k in range(STRIPS):
                    strip = slice(k * STRIP, (k + 1) * STRIP)
                    act.activation(strip_bias[strip, :], biases[strip, k % 2:k % 2 + 1], ACT.Copy).then_inc(bias_done, 1)

                def spread(b, r):
                    act.wait_ge(t_done, b + 1)
                    at = slice(b, b + 1) if b.__class__ is int else bass.ds(b, 1)
                    act.activation(xhat[:, at, :, 0:CH], ps_t[:, r, :].rearrange("p (a c t) -> p a c t", a=1, t=CH),
                                   ACT.Copy).then_inc(xhat_done, 1)

                for r in range(2):
                    spread(r, r)
                act.wait_ge(bias_done, STRIPS)
                with nc.scalar.Fori(0, B // 4 - 1) as h:
                    for r in range(2):
                        for rr in range(2):
                            spread(h * 4 + (2 * r + rr + 2), rr)
                        act.wait_ge(gates_mm, h * 2 + (r + 1))
                        act.activation(sig[:, bass.ds(h * 2 + r, 1), :], ps_g[:, r:r + 1, :], ACT.Sigmoid,
                                       bias=strip_bias[:]).then_inc(sig_done, 1)
                for rr in range(2):
                    spread(B - 2 + rr, rr)
                for m in (B // 2 - 2, B // 2 - 1):
                    act.wait_ge(gates_mm, m + 1)
                    act.activation(sig[:, m, :], ps_g[:, m % 2, :], ACT.Sigmoid, bias=strip_bias[:]).then_inc(sig_done, 1)
                act.wait_ge(gate_mm, 1)
                act.activation(gate[:].rearrange("p b c -> p (b c)"), ps_w[:, 3, :], ACT.Sigmoid,
                               bias=biases[:, 2:3]).then_inc(gate_done, 1)

            @block.gpsimd
            def _(pool):
                pool.memset(ident[:], 0.0).then_inc(consts, 1)
                pool.memset(ones[:], 1.0).then_inc(consts, 1)
                pool.memset(neghalf[:], -0.5).then_inc(consts, 1)
                pool.memset(halfmask[:], 1.0 / CH).then_inc(consts, 1)
                pool.memset(strips[:], 1.0 / (CH * STRIP)).then_inc(consts, 1)
                pool.wait_ge(consts, 5)
                pool.affine_select(out=ident[:], in_=ident[:], compare_op=ALU.not_equal, fill=1.0, base=0,
                                   pattern=[[-1, P]], channel_multiplier=1).then_inc(consts, 1)
                pool.affine_select(out=halfmask[:, 0:1], in_=halfmask[:, 0:1], compare_op=ALU.is_ge, fill=0.0,
                                   base=CH - 1, pattern=[[0, 1]], channel_multiplier=-1).then_inc(consts, 1)
                pool.affine_select(out=halfmask[:, 1:2], in_=halfmask[:, 1:2], compare_op=ALU.is_ge, fill=0.0,
                                   base=-CH, pattern=[[0, 1]], channel_multiplier=1).then_inc(consts, 1)
                pool.affine_select(out=strips[:], in_=strips[:], compare_op=ALU.is_ge, fill=0.0, base=0,
                                   pattern=[[-STRIP, STRIPS]], channel_multiplier=1).then_inc(consts, 1)
                pool.wait_ge(consts, 9)
                pool.affine_select(out=strips[:], in_=strips[:], compare_op=ALU.is_ge, fill=0.0, base=STRIP - 1,
                                   pattern=[[STRIP, STRIPS]], channel_multiplier=-1).then_inc(consts, 1)
                for q in range(QUARTERS):
                    at = quarter(q)
                    pool.wait_ge(vareps_done, q + 1)
                    pool.tensor_tensor(rstd[:, at], vareps[:, at], neghalf[:, at], ALU.pow).then_inc(rstd_done, 1)
                    pool.wait_ge(rstd_done, q + 1)
                    pool.tensor_tensor(sumsq[:, 0, at], meanvar[:, at, 1], rstd[:, at], ALU.mult).then_inc(sumsq_step, 1)
                    pool.wait_ge(sumsq_step, 3 * q + 1)
                    pool.tensor_tensor(sumsq[:, 1, at], sumsq[:, 0, at], rstd[:, at], ALU.mult).then_inc(sumsq_step, 1)
                    pool.wait_ge(sumsq_step, 3 * q + 2)
                    pool.tensor_scalar(sumsq[:, 2, at], sumsq[:, 1, at], float(D), 1e-10, ALU.mult, ALU.max)\
                        .then_inc(sumsq_step, 1)
                    pool.wait_ge(sumsq_step, 3 * q + 3)
                    pool.tensor_tensor(kinv[:, at], sumsq[:, 2, at], neghalf[:, at], ALU.pow).then_inc(kinv_done, 1)
                    halves = halfmask[:].rearrange("p (a h) -> p a h", a=1).broadcast_to([P, TQ, HALVES])
                    pool.wait_ge(kinv_done, q + 1)
                    pool.tensor_tensor(key_w[:, at, 0, :], kinv[:, at].rearrange("p (i a) -> p i a", a=1)
                                       .broadcast_to([P, TQ, HALVES]), halves, ALU.mult).then_inc(key_w_done, 1)
                    pool.wait_ge(key_w_done, 2 * q + 1)
                    pool.tensor_tensor(key_w[:, at, 1, :], halves, key_w[:, at, 0, :], ALU.subtract).then_inc(key_w_done, 1)
                later_constants(pool)

            @block.tensor
            def _(pe):
                def mean_keys(b):
                    pe.wait_ge(key_w_done, 2 * (b * TPB // TQ) + 2)
                    for i in range(b * TPB, (b + 1) * TPB):
                        mm = pe.matmul(ps_k[:, i].rearrange("p k h -> p (k h)"), xn[:, i, :],
                                       key_w[:, i].rearrange("p k h -> p (k h)"), start=True, stop=True)
                    if b == B - 1:
                        mm.then_inc(key_mm, 1)

                def gates(m):
                    pe.wait_ge(xhat_done, 2 * m + 2)
                    if m == 0:
                        pe.wait_ge(rep_done, REPS)
                    if m >= 2:
                        pe.wait_ge(sig_done, m - 1)
                    for k in range(STRIPS):
                        mm = pe.matmul(ps_g[k * STRIP:(k + 1) * STRIP, m % 2, :], token_rep[:, k % 2, :],
                                       xhat[:, 2 * m + k // 2, :, 0:CH], start=True, stop=True)
                    mm.then_inc(gates_mm, 1)

                pe.wait_ge(consts, 10)
                for b in range(B):
                    pe.wait_ge(xn_done, b + 1)
                    if b >= 2:
                        pe.wait_ge(xhat_done, b - 1)
                    for j in range(TPB):
                        mm = pe.transpose(ps_t[:, b % 2, j * P:(j + 1) * P], xn[:, b * TPB + j, :], ident[:])
                    mm.then_inc(t_done, 1)
                    if b == 0:
                        pe.wait_ge(w_in, 16 * 9)
                        for n in range(3):
                            mm = pe.transpose(ps_w[:, n, :], raw_w[:, n, :], ident[:])
                        mm.then_inc(wt_done, 1)
                    else:
                        mean_keys(b - 1)
                        if b % 2 == 0:
                            gates(b // 2 - 1)
                mean_keys(B - 1)
                gates(B // 2 - 1)
                pe.wait_ge(key_done, 2)
                pe.matmul(ps_w[:, 3, :], gate_rep[:], key[:].rearrange("p b c -> p (b c)"), start=True, stop=True)\
                  .then_inc(gate_mm, 1)
                pe.wait_ge(sum_done, 2)
                for k in range(STRIPS):
                    mm = pe.matmul(ps_b[:, k].rearrange("p m c -> p (m c)"), select[:, k, :],
                                   sig_sum[:].rearrange("p m c -> p (m c)"), start=True, stop=True)
                mm.then_inc(means_mm, 1)

            @block.vector
            def _(dve):
                def statistics(q):
                    dve.wait_ge(x_in[q], 16)
                    for i in range(q * TQ, (q + 1) * TQ):
                        dve.bn_stats(stats[:, i, :], x_tok[:, i, :]).then_inc(stat_done, 1)
                    for i in range(q * TQ, (q + 1) * TQ):
                        dve.wait_ge(stat_done, i + 1)
                        dve.bn_aggr(meanvar[:, i, :], stats[:, i, :]).then_inc(mean_done, 1)
                    dve.wait_ge(mean_done, (q + 1) * TQ)
                    dve.tensor_scalar(vareps[:, quarter(q)], meanvar[:, quarter(q), 1], EPS, None, ALU.add)\
                       .then_inc(vareps_done, 1)

                def normalise(q):
                    dve.wait_ge(rstd_done, q + 1)
                    for i in range(q * TQ, (q + 1) * TQ):
                        ins = dve.tensor_scalar(xn[:, i, :], x_tok[:, i, :], meanvar[:, i, 0:1], rstd[:, i:i + 1],
                                                ALU.subtract, ALU.mult)
                        if i % TPB == TPB - 1:
                            ins.then_inc(xn_done, 1)

                statistics(0)
                for q in range(QUARTERS):
                    if q < QUARTERS - 1:
                        statistics(q + 1)
                    normalise(q)
                    if q == 0:
                        dve.wait_ge(wt_done, 1)
                        for n, w in enumerate((minit_t, w1t, w2t)):
                            dve.tensor_copy(w[:], ps_w[:, n, :]).then_inc(wt_copied, 1)
                        dve.tensor_scalar(gate_rep[:], ones[:], vecs[:, 2:3], None, ALU.mult).then_inc(rep_done, 1)
                        for n in range(2):
                            dve.tensor_scalar(token_rep[:, n, :], ones[:, 0:STRIP], vecs[:, n:n + 1], None, ALU.mult)\
                               .then_inc(rep_done, 1)
                        for k in range(STRIPS):
                            dve.tensor_scalar(select[:, k, :], ones[:], strips[:, k:k + 1], None, ALU.mult)\
                               .then_inc(rep_done, 1)
                for part in range(2):
                    at = slice(part * B // 4, (part + 1) * B // 4)
                    dve.wait_ge(sig_done, (part + 1) * B // 4)
                    dve.tensor_reduce(sig_sum[:, at], sig[:, at].rearrange("p m (c t) -> p m c t", t=CH), AX.X, ALU.add)\
                       .then_inc(sum_done, 1)
                dve.wait_ge(key_mm, 1)
                means = ps_k[:].rearrange("p (b i) k h -> p k b i h", b=B)
                dve.tensor_copy(key[:].rearrange("p b (i h) -> p b i h", h=HALVES), means[:, 0]).then_inc(key_done, 1)
                dve.tensor_copy(xhat[:, :, :, CH].rearrange("p b (i h) -> p b i h", h=HALVES), means[:, 1])\
                   .then_inc(key_done, 1)
                dve.wait_ge(means_mm, 1)
                sigmoids = ps_b[:].rearrange("p (j n) m c -> p n m j c", n=2)
                dve.tensor_scalar(eta[:].rearrange("p (m j) c -> p m j c", j=2), sigmoids[:, 0], 0.2, None, ALU.mult)\
                   .then_inc(coef_step, 1)
                dve.tensor_scalar(alpha[:].rearrange("p (m j) c -> p m j c", j=2), sigmoids[:, 1], 0.5, 0.5, ALU.mult,
                                  ALU.add).then_inc(coef_step, 1)
                dve.wait_ge(gate_done, 1)
                dve.wait_ge(coef_step, 2)
                dve.tensor_tensor(coef_err[:].rearrange("p c b -> p b c"), gate[:], eta[:], ALU.mult).then_inc(coef_step, 1)
                dve.tensor_tensor(alpha[:], gate[:], alpha[:], ALU.mult).then_inc(coef_step, 1)
                dve.wait_ge(coef_step, 4)
                dve.tensor_scalar(gate[:], gate[:], -1.0, 1.0, ALU.mult, ALU.add).then_inc(coef_step, 1)
                dve.wait_ge(coef_step, 5)
                dve.tensor_tensor(coef_keep[:].rearrange("p c b -> p b c"), gate[:], alpha[:], ALU.add).then_inc(coef_step, 1)

        with ExitStack() as c3:
            def sb3(name, shape, dt=F32):
                return c3.enter_context(nc.sbuf_tensor(name, shape, dt))

            def sems(name):
                return [c3.enter_context(nc.semaphore(f"{name}{g}")) for g in range(G)]

            y = sb3("y", [P, G, GB, CH])
            hid = sb3("hid", [P, G, GB * CH])
            lead = sb3("lead", [P, G, GB])
            hsum = sb3("hsum", [P, G, GB])
            err = sb3("err", [P, G, GB])
            err_s = sb3("err_s", [P, G, GB])
            diag = sb3("diag", [P, G, GB, D])
            mta = sb3("mta", [P, B, D])
            sq = sb3("sq", [P, G, 2, D])
            ssq = sb3("ssq", [P, G, GB])
            norm2 = sb3("norm2", [P, G, GB])
            norm = sb3("norm", [P, G, GB])
            norm_inv = sb3("norm_inv", [P, G, GB])
            scale = sb3("scale", [P, G, GB])
            keep = sb3("keep", [P, G, GB])
            half = sb3("half", [P, GB])
            ps_y = [c3.enter_context(nc.psum_tensor(f"ps_y{g}", [P, 2, 512], F32)) for g in range(G)]
            ps_h = [c3.enter_context(nc.psum_tensor(f"ps_h{g}", [P, 512], F32)) for g in range(G)]
            ps_v = [c3.enter_context(nc.psum_tensor(f"ps_v{g}", [P, 512], F32)) for g in range(G)]
            start_done = c3.enter_context(nc.semaphore("start_done"))
            mt_done, y_mm, y_done, lead_done, h_mm, h_done, hsum_done, hs_mm, v_mm, v_done = (
                sems(n) for n in ("mt_done", "y_mm", "y_done", "lead_done", "h_mm", "h_done", "hsum_done", "hs_mm",
                                  "v_mm", "v_done"))
            err_done, errs_done, diag_done, spread_mm, keep_done, mta_done, ssq_done = (
                sems(n) for n in ("err_done", "errs_done", "diag_done", "spread_mm", "keep_done", "mta_done", "ssq_done"))
            norm_mm, norm_c, norm_done, ninv_a, ninv_b, scale_done = (
                sems(n) for n in ("norm_mm", "norm_c", "norm_done", "ninv_a", "ninv_b", "scale_done"))
            block = c3.enter_context(nc.Block())

            HB = GB // 2

            def y_part(g, lo, hi):
                return ps_y[g][:, :, 0:HB * CW].rearrange("p k (b t) -> p k b t", t=CW)[:, :, :, lo:hi]

            def steps(engine, body):
                body(0, True, False)
                with engine.Fori(1, NCH - 1) as c:
                    body(c, False, False)
                body(NCH - 1, False, True)

            def at(c):
                return slice(c, c + 1) if c.__class__ is int else bass.ds(c, 1)

            @block.tensor
            def _(pe):
                pe.wait_ge(start_done, 2)

                def second(g, c):
                    pe.wait_ge(h_done[g], c + 1)
                    pe.matmul(ps_v[g][:], w2t[:], hid[:, g], start=True, stop=True).then_inc(v_mm[g], 1)

                def sums(g, c):
                    pe.wait_ge(hsum_done[g], c + 1)
                    pe.matmul(ps_h[g][:, 0:GB], w2t[:], hsum[:, g], start=True, stop=True).then_inc(hs_mm[g], 1)

                def body(c, first, last):
                    for g in range(G):
                        if not first:
                            pe.wait_ge(ssq_done[g], c * GB)
                            pe.matmul(ps_h[g][:, 0:GB], ones[:], ssq[:, g, :], start=True, stop=True).then_inc(norm_mm[g], 1)
                            pe.wait_ge(mt_done[g], c * GB)
                        for b in range(GB):
                            mm = pe.matmul(ps_y[g][:, b // HB, (b % HB) * CW:(b % HB + 1) * CW], mt[:, g * GB + b, :],
                                           xhat[:, g * GB + b, at(c), :], start=True, stop=True)
                        mm.then_inc(y_mm[g], 1)
                    for g in range(G):
                        pe.wait_ge(y_done[g], c + 1)
                        pe.matmul(ps_h[g][:], w1t[:], y[:, g].rearrange("p b t -> p (b t)"), start=True, stop=True)\
                          .then_inc(h_mm[g], 1)
                    if not last:
                        sums(0, c)
                    second(0, c)
                    if last:
                        second(1, c)
                    else:
                        for g in range(G):
                            if g == 1:
                                second(g, c)
                            pe.wait_ge(diag_done[g], c + 1)
                            for k in range(2):
                                mm = pe.matmul(ps_y[g][:, k, :], ones[:],
                                               diag[:, g, k * HB:(k + 1) * HB, :].rearrange("p b d -> p (b d)"),
                                               start=True, stop=True)
                                mm.then_inc(spread_mm[g], 1)
                                if g == 0 and k == 0:
                                    sums(1, c)

                steps(nc.tensor, body)

            @block.scalar
            def _(act):
                def squared_norms(g, c):
                    act.wait_ge(norm_mm[g], c)
                    act.activation(norm2[:, g], ps_h[g][:, 0:GB], ACT.Copy).then_inc(norm_c[g], 1)

                def body(c, first, last):
                    if not first:
                        for g in range(G):
                            for b in range(GB):
                                if g == 1 and b == 3:
                                    squared_norms(0, c)
                                act.wait_ge(mt_done[g], c * GB + (b + 1 - GB))
                                if b >= 2:
                                    act.wait_ge(ssq_done[g], c * GB + (b - 1 - GB))
                                act.activation(sq[:, g, b % 2, :], mt[:, g * GB + b, :], ACT.Square,
                                               accum_out=ssq[:, g, b:b + 1]).then_inc(ssq_done[g], 1)
                        squared_norms(1, c)
                    for g in range(G):
                        act.wait_ge(h_mm[g], c + 1)
                        if not first:
                            act.wait_ge(v_mm[g], c)
                        act.activation(hid[:, g], ps_h[g][:], ACT.Silu).then_inc(h_done[g], 1)

                steps(nc.scalar, body)

            @block.gpsimd
            def _(pool):
                pool.memset(half[:], 0.5).then_inc(start_done, 1)

                def body(c, first, last):
                    if not first:
                        for g in range(G):
                            pool.wait_ge(norm_c[g], c)
                            pool.tensor_tensor(norm[:, g], norm2[:, g], half[:], ALU.pow).then_inc(norm_done[g], 1)
                    for g in range(G):
                        if last:
                            continue
                        if not first:
                            pool.wait_ge(scale_done[g], c)
                            pool.tensor_tensor(keep[:, g:g + 1], coef_keep[:, at(c), g * GB:(g + 1) * GB], scale[:, g:g + 1],
                                               ALU.mult).then_inc(keep_done[g], 1)
                            pool.wait_ge(keep_done[g], c)
                            factor = keep[:, g]
                        else:
                            pool.wait_ge(start_done, 2)
                            factor = coef_keep[:, 0, g * GB:(g + 1) * GB]
                        pool.tensor_tensor(mta[:, g * GB:(g + 1) * GB, :], mt[:, g * GB:(g + 1) * GB, :],
                                           factor.rearrange("p (b a) -> p b a", a=1).broadcast_to([P, GB, D]),
                                           ALU.mult).then_inc(mta_done[g], 1)

                pool.wait_ge(start_done, 1)
                steps(nc.gpsimd, body)

            @block.vector
            def _(dve):
                dve.wait_ge(start_done, 1)
                dve.tensor_copy(mt[:], minit_t[:].rearrange("p (a d) -> p a d", a=1).broadcast_to([P, B, D]))\
                   .then_inc(start_done, 1)

                def outputs(g, c, done):
                    dve.wait_ge(v_mm[g], done)
                    dve.wait_ge(y_done[g], done)
                    dve.tensor_tensor(vg_t[:, g * GB:(g + 1) * GB, bass.ds(c * CH, CH)],
                                      ps_v[g][:].rearrange("p (b t) -> p b t", t=CH), y[:, g], ALU.add)\
                       .then_inc(v_done[g], 1)

                def body(c, first, last):
                    for g in range(G):
                        if not first:
                            dve.wait_ge(norm_done[g], c)
                            dve.tensor_scalar(norm_inv[:, g], norm[:, g], 1e-6, None, ALU.add).then_inc(ninv_a[g], 1)
                            dve.wait_ge(ninv_a[g], c)
                            dve.reciprocal(norm_inv[:, g], norm_inv[:, g]).then_inc(ninv_b[g], 1)
                            dve.wait_ge(ninv_b[g], c)
                            dve.tensor_scalar(scale[:, g], norm_inv[:, g], 30.0, 1.0, ALU.mult, ALU.min)\
                               .then_inc(scale_done[g], 1)
                        dve.wait_ge(y_mm[g], c + 1)
                        out_y = y[:, g].rearrange("p (k b) t -> p k b t", k=2)
                        out_lead = lead[:, g].rearrange("p (k b a) -> p k b a", k=2, a=1)
                        if first:
                            dve.tensor_copy(out_y, y_part(g, 0, CH)).then_inc(y_done[g], 1)
                            dve.tensor_copy(out_lead, y_part(g, CH, CW)).then_inc(lead_done[g], 1)
                        else:
                            dve.wait_ge(v_done[g], c)
                            dve.wait_ge(scale_done[g], c)
                            s = scale[:, g].rearrange("p (k b a) -> p k b a", k=2, a=1)
                            dve.tensor_tensor(out_y, y_part(g, 0, CH), s.broadcast_to([P, 2, HB, CH]), ALU.mult)\
                               .then_inc(y_done[g], 1)
                            dve.tensor_tensor(out_lead, y_part(g, CH, CW), s, ALU.mult).then_inc(lead_done[g], 1)

                    def error(g):
                        dve.wait_ge(hs_mm[g], c + 1)
                        dve.wait_ge(lead_done[g], c + 1)
                        dve.scalar_tensor_tensor(out=err[:, g], in0=ps_h[g][:, 0:GB], scalar=1.0 / CH, in1=lead[:, g],
                                                 op0=ALU.mult, op1=ALU.add).then_inc(err_done[g], 1)
                        dve.wait_ge(err_done[g], c + 1)
                        dve.tensor_tensor(err_s[:, g:g + 1], err[:, g:g + 1], coef_err[:, at(c), g * GB:(g + 1) * GB],
                                          ALU.mult).then_inc(errs_done[g], 1)
                        dve.wait_ge(errs_done[g], c + 1)
                        dve.tensor_tensor(diag[:, g], ident[:].rearrange("p (a d) -> p a d", a=1).broadcast_to([P, GB, D]),
                                          err_s[:, g].rearrange("p (b a) -> p b a", a=1).broadcast_to([P, GB, D]),
                                          ALU.mult).then_inc(diag_done[g], 1)

                    def update(g):
                        dve.wait_ge(mta_done[g], c + 1)
                        if not first:
                            dve.wait_ge(ssq_done[g], c * GB)
                        for b in range(GB):
                            if b % HB == 0:
                                dve.wait_ge(spread_mm[g], c * 2 + (b // HB + 1))
                            dve.scalar_tensor_tensor(
                                out=mt[:, g * GB + b, :], in0=ps_y[g][:, b // HB, (b % HB) * D:(b % HB + 1) * D],
                                scalar=key[:, g * GB + b, at(c)], in1=mta[:, g * GB + b, :],
                                op0=ALU.mult, op1=ALU.add).then_inc(mt_done[g], 1)

                    if not last:
                        for g in range(G):
                            dve.wait_ge(h_done[g], c + 1)
                            dve.tensor_reduce(hsum[:, g], hid[:, g].rearrange("p (b t) -> p b t", t=CH), AX.X, ALU.add)\
                               .then_inc(hsum_done[g], 1)
                            error(g)
                    outputs(0, c, c + 1)
                    if last:
                        outputs(1, c, c + 1)
                    else:
                        update(0)
                        update(1)
                        outputs(1, c, c + 1)

                steps(nc.vector, body)


def attention_program(nc, io, x_tok, vg_t, ident, ones, rows_dram, SEG, row_w, count, passed_by, loaded):
    B, S, D = io.x.shape
    H = N_HEAD
    HD = D // H
    SCALE = HD ** -0.5
    T = S // P
    PAIRS = H // 2
    LOADS = 14 + 2 * io.W1.shape[0]
    QUADS = H // 4
    TERMS = PRODUCTS
    HROWS = TERMS * HD
    PROWS = 2 * HROWS
    SHIFTS = SPLIT
    KROWS = PROWS + 2 * SHIFTS
    Q_PARTS = (0, 0, 1, 0, 1, 2)
    K_PARTS = (1, 0, 0, 2, 1, 0)
    SLOTS = 32
    UNITS = 64
    EXP_STEP = 2
    BANKS = 3
    VW = VALUE_W
    RING = 4
    E = io.W1.shape[0]

    MISC = (("mx1", 1, 0), ("vg", 3, 2), ("o3", 5, -1), ("at", 7, -1), ("z", 9, 2), ("wo", 11, -1), ("q", 13, 2),
            ("k", 15, 2), ("v", 17, 2), ("mx0", 19, 1), ("o0", 21, 0), ("o1", 23, 0), ("rk", 27, -1), ("o2", 29, 0))
    MIDDLE = 18
    LOOP_FROM, LOOP_TO = 2, 14
    FIRST, LAST = -2, B

    def valid(i, d):
        return 0 <= i + d < B

    def uses_before(i, name):
        order = [n for n, _, _ in MISC]
        if i.__class__ is int:
            n = sum(valid(k, d) for k in range(FIRST, i) for _, _, d in MISC)
            return n + sum(valid(i, d) for _, _, d in MISC[:order.index(name)])
        return i * len(MISC) + (uses_before(LOOP_FROM, MISC[0][0]) + order.index(name) - LOOP_FROM * len(MISC))

    def used(i, name):
        if i.__class__ is int and not valid(i, [d for n, _, d in MISC if n == name][0]):
            return 0
        return uses_before(i, name) + 1

    def slot_of(name):
        return [s for n, s, _ in MISC if n == name][0]

    def wait(engine, semaphore, value):
        if value.__class__ is not int or value > 0:
            engine.wait_ge(semaphore, value)
            if engine.engine == mybir.EngineType.SP:
                engine.sem_inc(sp_passed, 1)

    def steps(engine, body):
        for i in range(FIRST, LOOP_FROM):
            body(i, i % 2)
        with engine.Fori(0, (LOOP_TO - LOOP_FROM) // 2) as n:
            for r in range(2):
                body(n * 2 + (LOOP_FROM + r), r)
        for i in range(LOOP_TO, LAST + 1):
            body(i, i % 2)

    def on(i, d):
        return i.__class__ is not int or valid(i, d)

    sp_passed, pool_passed, _ = passed_by

    with ExitStack() as ctx:
        def sb(name, shape, dt=F32):
            return ctx.enter_context(nc.sbuf_tensor("a_" + name, shape, dt))

        def sem(name):
            return ctx.enter_context(nc.semaphore("a_" + name))

        wq, wk, wv, wo, bqk, rows_b, router_b, w_in, ks, vaug, set_up = loaded
        vg_now = sb("vg_seq", [P, S])
        stats = sb("stats", [P, T, 6])
        mv = sb("mv", [P, T, 2])
        vareps = sb("vareps", [P, T])
        rstd = sb("rstd", [P, T])
        neghalf = sb("neghalf", [P, T])
        z = sb("z", [P, T, D])
        z_t = sb("z_t", [P, S])
        qk = sb("qk", [P, 2, S])
        parts = sb("parts", [P, 3, 2, S], BF16)
        qs = [sb(f"qs{r}", [P, PAIRS, S], BF16) for r in range(2)]
        v_c = [sb(f"v_c{r}", [P, T, D]) for r in range(2)]
        mx = sb("mx", [P, 2, H // 2 * T])
        mparts = sb("mparts", [H // 2 * T, 2, SHIFTS, P], BF16)
        mrest = sb("mrest", [H // 2 * T, P])
        prob = sb("prob", [P, RING, 4, S])
        o_t = sb("o_t", [P, 2, S])
        rden = sb("rden", [P, T, 4])
        attn = sb("attn", [P, T, H, HD])
        a_t = sb("a_t", [P, S])
        r_in = sb("r_in", [P, T, D])
        stats2 = sb("stats2", [P, T, 6])
        mv2 = sb("mv2", [P, T, 2])
        vareps2 = sb("vareps2", [P, T])
        rstd2 = sb("rstd2", [P, T])
        tnorm = sb("tnorm", [P, T, D])
        row = sb("row", [P, T, row_w])
        route = sb("route", [P, 3, T])
        route_i = sb("route_i", [P, 3, T], I32)
        e_iota = sb("e_iota", [P, T, E])
        hot = sb("hot", [P, 2 * T + 1, E])
        number = sb("number", [P, T])
        lower = sb("lower", [P, P])
        place = sb("place", [P, T, E])
        pos_i = sb("pos_i", [P, T], I32)

        stacks = nc.dram_tensor("stacks", (2, 2, H, TERMS, HD, S), BF16, kind="Internal").ap()
        maxima = nc.dram_tensor("maxima", (2, 2, SHIFTS, PAIRS // 2 * T, P), BF16, kind="Internal").ap()

        ps_s = ctx.enter_context(nc.psum_tensor("ps_s", [P, BANKS, S], F32))
        ps_x = ctx.enter_context(nc.psum_tensor("ps_x", [P, BANKS, S], F32))
        ps_o = ctx.enter_context(nc.psum_tensor("ps_o", [P, S], F32))
        ps_m = ctx.enter_context(nc.psum_tensor("ps_m", [P, S], F32))

        consts = sem("consts")
        misc_full = sem("misc_full")
        misc_free = sem("misc_free")
        vg_copied = sem("vg_copied")
        stat_done = sem("stat_done")
        vareps_done = sem("vareps_done")
        mean_done = sem("mean_done")
        rstd_done = sem("rstd_done")
        z_done = sem("z_done")
        zb_done = sem("zb_done")
        split_step = sem("split_step")
        spilled = sem("spilled")
        qk_done = sem("qk_done")
        middle_done = sem("middle_done")
        mspilled = [sem("mspilled0"), sem("mspilled1")]
        st0_in = sem("st0_in")
        st1_in = sem("st1_in")
        vaug_done = sem("vaug_done")
        mx_mm = sem("mx_mm")
        max_done = sem("max_done")
        msplit_step = sem("msplit_step")
        sh0_in = sem("sh0_in")
        sh1_in = sem("sh1_in")
        qk_mm = sem("qk_mm")
        exp_done = sem("exp_done")
        pv_mm = sem("pv_mm")
        o_done = sem("o_done")
        rden_done = sem("rden_done")
        stat2_done = sem("stat2_done")
        mean2_done = sem("mean2_done")
        vareps2_done = sem("vareps2_done")
        rstd2_done = sem("rstd2_done")
        tnorm_done = sem("tnorm_done")
        x2_step = sem("x2_step")
        x2_done = sem("x2_done")
        kprod_done = sem("kprod_done")
        res_done = sem("res_done")
        keys_done = sem("keys_done")
        route_step = sem("route_step")
        hot_done = sem("hot_done")
        place_step = sem("place_step")
        pos_done = sem("pos_done")
        scattered = sem("scattered")
        block = ctx.enter_context(nc.Block())

        bv, bo, ln_g, ln_b, rw = (rows_b[:, n, :] for n in range(5))
        CONSTS = 8
        STACKS = 3 * 16
        SHIFTED = 16
        SPILLS = 2 * TERMS * 16

        def tokens(b):
            return slice(b * T, b * T + T) if b.__class__ is int else bass.ds(b * T, T)

        def tile_of(b, t):
            return slice(b * T + t, b * T + t + 1) if b.__class__ is int else bass.ds(b * T + t, 1)

        def seq(b):
            return slice(b, b + 1) if b.__class__ is int else bass.ds(b, 1)

        def by_tile(ap):
            return ap.rearrange("p (t d) -> p t d", d=D)

        def bcast_rows(ap):
            return ap.rearrange("p (a d) -> p a d", a=1).broadcast_to([P, T, D])

        @block.sync
        def _(sp):
            def spill(b, r):
                for side, order in enumerate((Q_PARTS, K_PARTS)):
                    for n in range(TERMS):
                        sp.dma_start(stacks[r, side, :, n, :, :], parts[:, order[n], side, :]).then_inc(spilled, 16)

            def stack(r, half, landed):
                pairs = slice(half * PAIRS // 2, (half + 1) * PAIRS // 2)
                rows = stacks.rearrange("r s (pr hh) n d t -> r s hh (n d) pr t", hh=2)
                both = stacks.rearrange("r s (pr hh) n d t -> r s (hh n d) pr t", hh=2)
                sp.dma_start(qs[r][0:PROWS, pairs, :], both[r, 0, :, pairs, :]).then_inc(landed, 16)
                for hh in range(2):
                    sp.dma_start(ks[r][:].rearrange("p (pr hh) t -> p pr hh t", hh=2)[HROWS * hh:HROWS * (hh + 1), pairs, hh, :],
                                 rows[r, 1, hh, :, pairs, :]).then_inc(landed, 16)

            def spill_maxima(half):
                own = PAIRS // 2 * T
                for hh in range(2):
                    sp.dma_start(maxima[half, hh].rearrange("n m t -> m n t"), mparts[own * hh:own * (hh + 1), half])\
                      .then_inc(mspilled[half], 16)

            def shift(b, r, half, landed):
                wait(sp, mspilled[half], 32 * (b + 1))
                sp.dma_start(qs[r][PROWS:KROWS, half * PAIRS // 2:(half + 1) * PAIRS // 2, :],
                             maxima[half].rearrange("hh n (pr q) t -> (hh n) pr (q t)", q=T)).then_inc(landed, 16)

            def body(i, r):
                if on(i, 0):
                    wait(sp, msplit_step, 3 * (2 * i + 2))
                    spill_maxima(1)
                if on(i, 1):
                    wait(sp, spilled, SPILLS * (i + 2))
                    wait(sp, qk_mm, i * UNITS)
                    stack(1 - r, 1, st1_in)
                if on(i, 0):
                    shift(i, r, 1, sh1_in)
                if on(i, 2):
                    wait(sp, split_step, 2 * (i + 3))
                    spill(i + 2, r)
                if on(i, 1):
                    wait(sp, msplit_step, 3 * (2 * i + 3))
                    spill_maxima(0)
                    shift(i + 1, 1 - r, 0, sh0_in)
                if on(i, 2):
                    wait(sp, qk_mm, i * UNITS + UNITS // 2)
                    wait(sp, spilled, SPILLS * (i + 3))
                    stack(r, 0, st0_in)

            steps(nc.sync, body)
            sp.wait_ge(st0_in, STACKS * B)
            sp.wait_ge(st1_in, STACKS * B)

        @block.tensor
        def _(pe):
            pe.wait_ge(set_up, 2 + 4 * 16)
            pe.wait_ge(w_in, 16 * LOADS)
            pe.wait_ge(consts, CONSTS)

            def misc(i, r, name):
                wait(pe, misc_free, uses_before(i, name))
                tiles = [slice(t * P, (t + 1) * P) for t in range(T)]
                if name == "vg":
                    wait(pe, vg_copied, i + 3)
                    for t in tiles:
                        mm = pe.transpose(ps_m[:, t], vg_now[:, t], ident[:])
                elif name == "z":
                    wait(pe, z_done, T * (i + 3))
                    for n, t in enumerate(tiles):
                        mm = pe.transpose(ps_m[:, t], z[:, n, :], ident[:])
                elif name in "qkv":
                    if name == "v":
                        for t in tiles:
                            mm = pe.matmul(ps_m[:, t], z_t[:, t], wv[:], start=True, stop=True)
                    else:
                        mm = pe.matmul(ps_m[:], (wq if name == "q" else wk)[:], z_t[:], start=True, stop=True)
                elif name[:2] == "mx":
                    half = int(name[2])
                    wait(pe, max_done, UNITS * (i + 1) if half else UNITS * (i + 1) + UNITS // 2)
                    mm = pe.transpose(ps_m[0:H // 2 * T, 0:P], mx[:, half, :], ident[:])
                elif name[0] == "o":
                    g = int(name[1])
                    wait(pe, o_done, QUADS * (i - 1) + g + 1 if g == 3 else QUADS * i + g + 1)
                    for t in tiles:
                        mm = pe.transpose(ps_m[:, t], o_t[:, g % 2, t], ident[:])
                elif name == "at":
                    for n, t in enumerate(tiles):
                        mm = pe.transpose(ps_m[:, t], attn[:, n].rearrange("p h d -> p (h d)"), ident[:])
                elif name == "wo":
                    for t in tiles:
                        mm = pe.matmul(ps_m[:, t], a_t[:, t], wo[:], start=True, stop=True)
                elif name == "rk":
                    wait(pe, hot_done, i)
                    ahead = hot[:].rearrange("p t e -> p (t e)")
                    for k in range(T + 1):
                        mm = pe.matmul(ps_m[:, 0:(T + 1) * E], (ones if k else lower)[:],
                                       ahead[:, (T - k) * E:(2 * T + 1 - k) * E], start=(k == 0), stop=(k == T))
                mm.then_inc(misc_full, 1)

            def bank_free(done, b, n, step=1):
                if n == 0:
                    wait(pe, done, b * (UNITS * step))
                elif n >= BANKS:
                    wait(pe, done, b * (UNITS * step) + (n + 1 - BANKS) * step)

            def maxima_of(i, r, n):
                h, qt = n // T, n % T
                bank_free(max_done, i + 1, n)
                pe.matmul(ps_x[:, n % BANKS, :], qs[1 - r][0:PROWS, h // 2, qt * P:(qt + 1) * P],
                          ks[1 - r][0:PROWS, h, :], start=True, stop=True).then_inc(mx_mm, 1)

            def values(b, r, v):
                g, kt = v // T, v % T
                wait(pe, exp_done, b * (UNITS * EXP_STEP) + (4 * v + 4) * EXP_STEP)
                if kt == 0:
                    wait(pe, o_done, QUADS * b + g)
                if v == 0:
                    wait(pe, vaug_done, b + 1)
                for j in range(4):
                    mm = pe.matmul(ps_o[32 * j:32 * j + VW, :], vaug[r][:, kt, 4 * g + j, :], prob[:, v % RING, j, :],
                                   start=(kt == 0), stop=(kt == T - 1))
                mm.then_inc(pv_mm, 1)

            def body(i, r):
                for s in range(SLOTS):
                    pair, kt = 2 * (s // 8) + s % 2, (s // 2) % T
                    if on(i, 1):
                        if s == 0:
                            wait(pe, st0_in, STACKS * (i + 2))
                        if s == SLOTS // 2:
                            wait(pe, st1_in, STACKS * (i + 2))
                    for hh in range(2):
                        if on(i, 1):
                            maxima_of(i, r, 2 * s + hh)
                        if on(i, 0):
                            if s == 0 and hh == 0:
                                wait(pe, sh0_in, SHIFTED * (i + 1))
                            if s == SLOTS // 2 and hh == 0:
                                wait(pe, sh1_in, SHIFTED * (i + 1))
                            bank_free(exp_done, i, 2 * s + hh, EXP_STEP)
                            pe.matmul(ps_s[:, (2 * s + hh) % BANKS, :], ks[r][0:KROWS, 2 * pair + hh, kt * P:(kt + 1) * P],
                                      qs[r][0:KROWS, pair, :], start=True, stop=True).then_inc(qk_mm, 1)
                    if s % 2 == 0:
                        if s < 4 and on(i, -1):
                            values(i - 1, 1 - r, 14 + s // 2)
                        if s >= 4 and on(i, 0):
                            values(i, r, s // 2 - 2)
                    for name, at, d in MISC:
                        if at == s and on(i, d):
                            misc(i, r, name)

            steps(nc.tensor, body)

        @block.scalar
        def _(act):
            act.wait_ge(w_in, 16 * LOADS)

            def body(i, r):
                for s in range(SLOTS):
                    for g, at, d in ((3, 3, -1), (0, 11, 0), (1, 19, 0), (2, 27, 0)):
                        if s == at and on(i, d):
                            b = i + d
                            act.wait_ge(pv_mm, b * (SLOTS // 2) + 4 * g + 4)
                            wait(act, misc_full, (used(i - 1, "o2"), used(i, "o3"), used(i, "o0"), used(i - 1, "o1"))[g])
                            act.activation(o_t[:, g % 2, :], ps_o[:], ACT.Copy).then_inc(o_done, 1)
                    if on(i, 0):
                        if s % 2 == 0:
                            wait(act, pv_mm, i * (SLOTS // 2) + s // 2 + 1 - RING)
                        for u in (2 * s, 2 * s + 1):
                            act.wait_ge(qk_mm, i * UNITS + u + 1)
                            act.activation(prob[:, (s // 2) % RING, u % 4, :], ps_s[:, u % BANKS, :],
                                           ACT.Exp, scale=SCALE).then_inc(exp_done, EXP_STEP)
                    if s == slot_of("z") and on(i, 2):
                        act.wait_ge(misc_full, used(i, "z"))
                        act.activation(z_t[:], ps_m[:], ACT.Copy).then_inc(misc_free, 1)
                    if s == slot_of("at") and on(i, -1):
                        act.wait_ge(misc_full, used(i, "at"))
                        act.activation(a_t[:], ps_m[:], ACT.Copy).then_inc(misc_free, 1)
                    for n, name in enumerate("qk"):
                        if s == slot_of(name) and on(i, 2):
                            act.wait_ge(misc_full, used(i, name))
                            if n == 0:
                                wait(act, split_step, 2 * (i + 2))
                            act.activation(qk[:, n, :], ps_m[:], ACT.Identity, bias=bqk[:, n:n + 1]).then_inc(qk_done, 1)
                            if n == 0:
                                wait(act, spilled, SPILLS * (i + 2))
                            act.activation(parts[:, 0, n, :], ps_m[:], ACT.Identity, bias=bqk[:, n:n + 1])\
                               .then_inc(misc_free, 1)
                    if s == MIDDLE and on(i, 2):
                        act.wait_ge(split_step, 2 * (i + 2) + 1)
                        act.activation(parts[:, 1], qk[:], ACT.Identity).then_inc(middle_done, 1)

            steps(nc.scalar, body)

        @block.gpsimd
        def _(pool):
            pool.memset(neghalf[:], -0.5).then_inc(consts, 1)
            pool.memset(hot[:], 0.0).then_inc(consts, 1)
            pool.memset(lower[:], 1.0).then_inc(consts, 1)
            pool.memset(row[:], 0.0).then_inc(consts, 1)
            pool.iota(e_iota[:], [[0, T], [1, E]], base=0, channel_multiplier=0, allow_small_or_imprecise_dtypes=True)\
                .then_inc(consts, 1)
            pool.iota(count[:], [[SEG, E]], base=0, channel_multiplier=0, allow_small_or_imprecise_dtypes=True)\
                .then_inc(consts, 1)
            pool.iota(number[:], [[P, T]], base=0, channel_multiplier=1, allow_small_or_imprecise_dtypes=True)\
                .then_inc(consts, 1)
            pool.wait_ge(consts, 7)
            pool.affine_select(out=lower[:], in_=lower[:], compare_op=ALU.is_gt, fill=0.0, base=0,
                               pattern=[[1, P]], channel_multiplier=-1).then_inc(consts, 1)
            pool.wait_ge(w_in, 16 * LOADS)

            def passed():
                pool.sem_inc(pool_passed, 1)

            def body(i, r):
                if on(i, 2):
                    wait(pool, misc_full, used(i - 1, "vg"))
                    passed()
                    pool.tensor_copy(vg_now[:].rearrange("p (a s) -> p a s", a=1), vg_t[:, seq(i + 2), :]).then_inc(vg_copied, 1)
                if on(i, 1):
                    wait(pool, misc_free, used(i - 1, "v"))
                    wait(pool, pv_mm, i * (SLOTS // 2))
                    passed()
                    pool.tensor_copy(vaug[1 - r][:, :, :, 0:HD],
                                     v_c[1 - r][:].rearrange("p t (h d) -> p t h d", d=HD)).then_inc(vaug_done, 1)
                if on(i, 2):
                    wait(pool, vareps_done, i + 3)
                    passed()
                    pool.tensor_tensor(rstd[:], vareps[:], neghalf[:], ALU.pow).then_inc(rstd_done, 1)
                    wait(pool, z_done, T * (i + 3))
                    wait(pool, vg_copied, i + 3)
                    passed()
                    pool.tensor_tensor(vg_t[:, seq(i + 2), :].rearrange("p a (t d) -> p (a t) d", d=D), z[:],
                                       bcast_rows(bo), ALU.add).then_inc(zb_done, 1)
                if on(i, -1):
                    wait(pool, vareps2_done, i)
                    passed()
                    pool.tensor_tensor(rstd2[:], vareps2[:], neghalf[:], ALU.pow).then_inc(rstd2_done, 1)
                if on(i, 2):
                    b = i + 2
                    flat = [parts[:, n].rearrange("p s t -> p (s t)") for n in range(3)]
                    left = qk[:].rearrange("p s t -> p (s t)")
                    pool.wait_ge(qk_done, 2 * b + 2)
                    passed()
                    pool.wait_ge(misc_free, used(i, "k"))
                    passed()
                    pool.tensor_tensor(left, left, flat[0], ALU.subtract).then_inc(split_step, 1)
                    pool.wait_ge(middle_done, b + 1)
                    passed()
                    pool.tensor_tensor(flat[2], left, flat[1], ALU.subtract).then_inc(split_step, 1)
                if on(i, -1):
                    wait(pool, scattered, 16 * T * (i - 1))
                    passed()
                    pool.tensor_copy(row[:, :, D:2 * D], x_tok[:, tokens(i - 1), :]).then_inc(res_done, 1)
                    pool.tensor_copy(row[:, :, 2 * D], number[:]).then_inc(res_done, 1)
                    wait(pool, tnorm_done, T * i)
                    passed()
                    pool.tensor_tensor(tnorm[:], tnorm[:], bcast_rows(ln_g), ALU.mult).then_inc(x2_step, 1)
                    pool.wait_ge(x2_step, 2 * i - 1)
                    passed()
                    pool.tensor_tensor(row[:, :, 0:D], tnorm[:], bcast_rows(ln_b), ALU.add).then_inc(x2_step, 1)
                    pool.wait_ge(x2_step, 2 * i)
                    passed()
                    pool.tensor_tensor(tnorm[:], row[:, :, 0:D], bcast_rows(rw), ALU.mult).then_inc(kprod_done, 1)
                    pool.wait_ge(res_done, 2 * i)
                    passed()
                    pool.tensor_scalar(number[:], number[:], float(S), 0.0, ALU.add, ALU.add).then_inc(x2_done, 1)
                    pool.wait_ge(pos_done, i)
                    pool.wait_ge(x2_done, i)
                    passed()
                    for t in range(T):
                        pool.indirect_dma_start(rows_dram, bass.IndirectOffsetOnAxis(ap=pos_i[:, t:t + 1], axis=0),
                                                row[:, t, :], None).then_inc(scattered, 16)

            steps(nc.gpsimd, body)
            pool.wait_ge(scattered, 16 * T * B)

        @block.vector
        def _(dve):
            dve.wait_ge(w_in, 16 * LOADS)
            dve.wait_ge(consts, CONSTS)

            def split_maxima(b, half, r, use):
                n = 2 * b + half
                rows = slice(0, H // 2 * T)
                dve.wait_ge(misc_full, use)
                wait(dve, (sh0_in, sh1_in)[half], SHIFTED * b)
                dve.tensor_copy(mparts[:, half, 0, :], ps_m[rows, 0:P]).then_inc(msplit_step, 1)
                dve.wait_ge(msplit_step, 3 * n + 1)
                dve.tensor_tensor(mrest[:], ps_m[rows, 0:P], mparts[:, half, 0, :], ALU.subtract).then_inc(misc_free, 1)
                dve.wait_ge(misc_free, use)
                dve.tensor_copy(mparts[:, half, 1, :], mrest[:]).then_inc(msplit_step, 1)
                dve.wait_ge(msplit_step, 3 * n + 2)
                dve.tensor_tensor(mparts[:, half, 2, :], mrest[:], mparts[:, half, 1, :], ALU.subtract)\
                   .then_inc(msplit_step, 1)

            def normalise_quad(b, g, use):
                dve.wait_ge(misc_full, use)
                sums = ps_m[:].rearrange("p (t j c) -> p t j c", t=T, c=VW)
                dve.reciprocal(rden[:].rearrange("p t (j a) -> p t j a", a=1), sums[:, :, :, HD:HD + 1]).then_inc(rden_done, 1)
                dve.wait_ge(rden_done, QUADS * b + g + 1)
                dve.tensor_tensor(attn[:, :, 4 * g:4 * g + 4, :], sums[:, :, :, 0:HD],
                                  rden[:].rearrange("p t (j a) -> p t j a", a=1).broadcast_to([P, T, 4, HD]),
                                  ALU.mult).then_inc(misc_free, 1)

            def body(i, r):
                for s in range(SLOTS):
                    if s == 2 and on(i, 0):
                        split_maxima(i, 1, r, used(i, "mx1"))
                    if s == 4 and on(i, 2):
                        dve.wait_ge(misc_full, used(i, "vg"))
                        dve.tensor_tensor(x_tok[:, tokens(i + 2), :], x_tok[:, tokens(i + 2), :], by_tile(ps_m[:]), ALU.add)\
                           .then_inc(misc_free, 1)
                    if s == 5 and on(i, 2):
                        for t in range(T):
                            dve.bn_stats(stats[:, t, :], x_tok[:, tile_of(i + 2, t), :]).then_inc(stat_done, 1)
                    if s == 6 and on(i, 2):
                        for t in range(T):
                            dve.bn_aggr(mv[:, t, :], stats[:, t, :]).then_inc(mean_done, 1)
                        dve.wait_ge(mean_done, T * (i + 3))
                        dve.tensor_scalar(vareps[:], mv[:, :, 1], EPS, None, ALU.add).then_inc(vareps_done, 1)
                    if s == 6 and on(i, -1):
                        normalise_quad(i - 1, 3, used(i, "o3"))
                    if s in (8, 9) and on(i, 2):
                        if s == 8:
                            dve.wait_ge(rstd_done, i + 3)
                            wait(dve, misc_full, used(i - 1, "z"))
                            wait(dve, zb_done, i + 2)
                        for t in range((s - 8) * T // 2, (s - 7) * T // 2):
                            dve.tensor_scalar(z[:, t:t + 1, :], x_tok[:, tile_of(i + 2, t), :], mv[:, t, 0:1], rstd[:, t:t + 1],
                                              ALU.subtract, ALU.mult).then_inc(z_done, 1)
                    if s == 12 and on(i, -1):
                        dve.wait_ge(misc_full, used(i, "wo"))
                        wait(dve, tnorm_done, T * (i - 1))
                        dve.tensor_tensor(r_in[:], vg_t[:, seq(i - 1), :].rearrange("p a (t d) -> p (a t) d", d=D),
                                          by_tile(ps_m[:]), ALU.add).then_inc(misc_free, 1)
                    if s == 13 and on(i, -1):
                        dve.wait_ge(misc_free, used(i, "wo"))
                        wait(dve, mean2_done, T * (i - 1))
                        for t in range(T):
                            dve.bn_stats(stats2[:, t, :], r_in[:, t, :]).then_inc(stat2_done, 1)
                    if s == 14 and on(i, -1):
                        for t in range(T):
                            dve.bn_aggr(mv2[:, t, :], stats2[:, t, :]).then_inc(mean2_done, 1)
                        dve.wait_ge(mean2_done, T * i)
                        dve.tensor_scalar(vareps2[:], mv2[:, :, 1], EPS, None, ALU.add).then_inc(vareps2_done, 1)
                    if s == 22 and on(i, 0):
                        normalise_quad(i, 0, used(i, "o0"))
                    if s == 18 and on(i, 2):
                        dve.wait_ge(misc_full, used(i, "v"))
                        wait(dve, vaug_done, i + 1)
                        dve.tensor_tensor(v_c[r][:], by_tile(ps_m[:]), bcast_rows(bv), ALU.add).then_inc(misc_free, 1)
                    if s in (16, 17) and on(i, -1):
                        if s == 16:
                            dve.wait_ge(rstd2_done, i)
                            wait(dve, keys_done, i - 1)
                        for t in range((s - 16) * T // 2, (s - 15) * T // 2):
                            dve.tensor_scalar(tnorm[:, t, :], r_in[:, t, :], mv2[:, t, 0:1], rstd2[:, t:t + 1],
                                              ALU.subtract, ALU.mult).then_inc(tnorm_done, 1)
                    if s == 20 and on(i, 1):
                        split_maxima(i + 1, 0, 1 - r, used(i, "mx0"))
                    if s == 24 and on(i, 0):
                        normalise_quad(i, 1, used(i, "o1"))
                    if s == 25 and on(i, -1):
                        n = 5 * (i - 1)
                        dve.wait_ge(kprod_done, i)
                        dve.tensor_reduce(route[:, 0, :], tnorm[:], AX.X, ALU.add).then_inc(route_step, 1)
                        dve.wait_ge(route_step, n + 1)
                        dve.tensor_scalar(route[:, 1, :], route[:, 0, :], router_b[:, 0:1], None, ALU.add)\
                           .then_inc(route_step, 1)
                        dve.wait_ge(route_step, n + 2)
                        dve.tensor_copy(route_i[:, 0, :], route[:, 1, :]).then_inc(route_step, 1)
                        dve.wait_ge(route_step, n + 3)
                        dve.tensor_tensor(route[:, 2, :], route_i[:, 0, :], route[:, 1, :], ALU.is_gt).then_inc(route_step, 1)
                        dve.wait_ge(route_step, n + 4)
                        dve.tensor_tensor(route_i[:, 1, :], route_i[:, 0, :], route[:, 2, :], ALU.subtract)\
                           .then_inc(route_step, 1)
                    if s == 26 and on(i, -1):
                        dve.wait_ge(route_step, 5 * i)
                        dve.tensor_scalar(route_i[:, 2, :], route_i[:, 1, :], E - 1, None, ALU.bitwise_and)\
                           .then_inc(keys_done, 1)
                        dve.wait_ge(keys_done, i)
                        dve.tensor_tensor(hot[:, T:2 * T, :], route_i[:, 2, :].rearrange("p (t a) -> p t a", a=1)
                                          .broadcast_to([P, T, E]), e_iota[:], ALU.is_equal).then_inc(hot_done, 1)
                    if s == 28 and on(i, -1):
                        ranks = ps_m[:, 0:(T + 1) * E].rearrange("p (t e) -> p t e", e=E)
                        dve.wait_ge(misc_full, used(i, "rk"))
                        wait(dve, scattered, 16 * T * (i - 1))
                        dve.tensor_tensor(place[:], ranks[:, 0:T, :], count[:].rearrange("p (a e) -> p a e", a=1)
                                          .broadcast_to([P, T, E]), ALU.add).then_inc(place_step, 1)
                        dve.wait_ge(place_step, 3 * i - 2)
                        dve.tensor_tensor(count[:], count[:], ranks[:, T, :], ALU.add).then_inc(misc_free, 1)
                        dve.wait_ge(misc_free, used(i, "rk"))
                        dve.tensor_tensor(place[:], place[:], hot[:, T:2 * T, :], ALU.mult).then_inc(place_step, 1)
                        dve.wait_ge(place_step, 3 * i - 1)
                        dve.tensor_reduce(route[:, 0, :], place[:], AX.X, ALU.add).then_inc(place_step, 1)
                        dve.wait_ge(place_step, 3 * i)
                        dve.tensor_copy(pos_i[:], route[:, 0, :]).then_inc(pos_done, 1)
                    if s == 30 and on(i, 0):
                        normalise_quad(i, 2, used(i, "o2"))
                    if s == 4 and on(i, 2):
                        dve.wait_ge(misc_free, used(i, "vg"))
                        wait(dve, mean_done, T * (i + 2))
                    if s == 5 and on(i, 2):
                        dve.wait_ge(stat_done, T * (i + 3))
                        wait(dve, z_done, T * (i + 2))
                    if s == 13 and on(i, -1):
                        dve.wait_ge(stat2_done, T * i)
                        wait(dve, tnorm_done, T * (i - 1))
                    if on(i, 1):
                        for n in (2 * s, 2 * s + 1):
                            h, qt = n // T, n % T
                            half = h // (H // 2)
                            col = (h % 2 * (PAIRS // 2) + h // 2 % (PAIRS // 2)) * T + qt
                            if n == 0:
                                wait(dve, misc_full, used(i - 1, "mx0"))
                            if n == UNITS // 2:
                                wait(dve, misc_full, used(i, "mx1"))
                            dve.wait_ge(mx_mm, UNITS * (i + 1) + n + 1)
                            dve.tensor_reduce(mx[:, half, col:col + 1], ps_x[:, n % BANKS, :], AX.X, ALU.max)\
                               .then_inc(max_done, 1)

            steps(nc.vector, body)


def experts_program(nc, io, ident, rows_dram, seg, row_w, block_w, count, passed_by, ln_gb, biases_all, out):
    B, S, D = io.x.shape
    E, _, F = io.W1.shape
    N = B * S
    NB = N // block_w + E - 1
    T = block_w // P
    FT = F // P
    RING = 3
    LOOPS = (NB - RING - 1) // RING
    assert NB == RING * (LOOPS + 1) + 1

    sp_passed, pool_passed, dve_passed = passed_by

    with ExitStack() as ctx:
        def sb(name, shape, dt=F32):
            return ctx.enter_context(nc.sbuf_tensor("e_" + name, shape, dt))

        def sem(name):
            return ctx.enter_context(nc.semaphore("e_" + name))

        padding = sb("padding", [P, T, row_w])
        numbers = sb("numbers", [P, T])
        seg_start = sb("seg_start", [P, E])
        block_no = sb("block_no", [P, NB])
        filled = sb("filled", [P, E])
        blocks_i = sb("blocks_i", [P, 3, E], I32)
        count_i = sb("count_i", [P, E], I32)
        n_blocks = sb("n_blocks", [P, E])
        ends = sb("ends", [P, E])
        passed_e = sb("passed_e", [P, NB, E])
        expert = sb("expert", [P, NB])
        first = sb("first", [P, NB])
        table = sb("table", [P, 2, NB], I32)
        work = sb("work", [P, 3, NB])
        neghalf = sb("neghalf", [P, T])
        rows = [sb(f"rows{r}", [P, T, row_w]) for r in range(RING)]
        w1 = [sb(f"w1{r}", [P, F]) for r in range(RING)]
        w2 = [sb(f"w2{r}", [P, FT, D]) for r in range(RING)]
        biases = [sb(f"biases{r}", [P, 1, FT + 1]) for r in range(RING)]
        x_t = [sb(f"x_t{r}", [P, block_w]) for r in range(RING)]
        hid = [sb(f"hid{r}", [P, FT, block_w]) for r in range(RING)]
        y_t = [sb(f"y_t{r}", [P, block_w]) for r in range(RING)]
        r_in = sb("r_in", [P, T, D])
        stats = sb("stats", [P, T, 6])
        mv = sb("mv", [P, T, 2])
        vareps = sb("vareps", [P, T])
        rstd = sb("rstd", [P, T])
        tn = sb("tn", [P, T, D])
        ids = [sb(f"ids{r}", [P, T], I32) for r in range(RING)]
        result = [sb(f"result{r}", [P, T, D]) for r in range(RING)]
        ps_a = ctx.enter_context(nc.psum_tensor("ps_a", [P, block_w], F32))
        ps_f = ctx.enter_context(nc.psum_tensor("ps_f", [P, FT, block_w], F32))
        ps_y = ctx.enter_context(nc.psum_tensor("ps_y", [P, block_w], F32))
        ps_b = ctx.enter_context(nc.psum_tensor("ps_b", [P, block_w], F32))

        consts = sem("consts")
        step = sem("step")
        table_done = sem("table_done")
        padded = sem("padded")
        rows_in = [sem(f"rows_in{r}") for r in range(RING)]
        weights_in = [sem(f"weights_in{r}") for r in range(RING)]
        xt_mm = sem("xt_mm")
        xt_done = sem("xt_done")
        hid_mm = sem("hid_mm")
        hid_done = sem("hid_done")
        y_mm = sem("y_mm")
        y_done = sem("y_done")
        back_mm = sem("back_mm")
        r_done = sem("r_done")
        stat_done = sem("stat_done")
        mean_done = sem("mean_done")
        vareps_done = sem("vareps_done")
        rstd_done = sem("rstd_done")
        tn_done = sem("tn_done")
        affine = sem("affine")
        result_done = sem("result_done")
        ids_done = sem("ids_done")
        sent = [sem(f"sent{r}") for r in range(RING)]
        block = ctx.enter_context(nc.Block())

        def wait(engine, semaphore, value):
            if value.__class__ is not int or value > 0:
                engine.wait_ge(semaphore, value)

        def blocks(engine, body):
            for j in range(RING):
                body(j, j, 0)
            with engine.Fori(0, LOOPS) as n:
                for r in range(RING):
                    body(n * RING + (RING + r), r, n + 1)
            body(NB - 1, 0, LOOPS + 1)

        def bcast(ap):
            return ap.rearrange("p (a d) -> p a d", a=1).broadcast_to([P, T, D])

        @block.gpsimd
        def _(pool):
            pool.memset(padding[:], 0.0).then_inc(consts, 1)
            pool.memset(neghalf[:], -0.5).then_inc(consts, 1)
            pool.iota(numbers[:], [[1, T]], base=N, channel_multiplier=T, allow_small_or_imprecise_dtypes=True).then_inc(consts, 1)
            pool.iota(seg_start[:], [[seg, E]], base=0, channel_multiplier=0, allow_small_or_imprecise_dtypes=True)\
                .then_inc(consts, 1)
            pool.iota(block_no[:], [[1, NB]], base=0, channel_multiplier=0, allow_small_or_imprecise_dtypes=True)\
                .then_inc(consts, 1)
            pool.wait_ge(consts, 5)
            pool.tensor_copy(padding[:, :, 2 * D], numbers[:]).then_inc(consts, 1)

            def body(j, r, before):
                pool.wait_ge(vareps_done, j + 1)
                pool.tensor_tensor(rstd[:], vareps[:], neghalf[:], ALU.pow).then_inc(rstd_done, 1)
                pool.wait_ge(result_done, j + 1)
                pool.wait_ge(ids_done, j + 1)
                pool.sem_inc(pool_passed, 1)
                for t in range(T):
                    pool.indirect_dma_start(out.rearrange("b s d -> (b s) d"),
                                            bass.IndirectOffsetOnAxis(ap=ids[r][:, t:t + 1], axis=0),
                                            result[r][:, t, :], None, bounds_check=N - 1, oob_is_err=False).then_inc(sent[r], 16)

            blocks(nc.gpsimd, body)
            for r in range(RING):
                pool.wait_ge(sent[r], 16 * T * ((NB - 1 - r) // RING + 1))

        @block.sync
        def _(sp):
            sp.wait_ge(consts, 6)
            for k in range(E - 1):
                sp.dma_start(rows_dram[E * seg + k * block_w:E * seg + (k + 1) * block_w, :]
                             .rearrange("(p t) w -> p t w", t=T), padding[:]).then_inc(padded, 16)
            sp.wait_ge(table_done, 1)
            for e in range(E):
                end = sp.value_load(count_i[0:1, e:e + 1], min_val=e * seg, max_val=e * seg + N)
                sp.dma_start(rows_dram[bass.ds(end, block_w), :].rearrange("(p t) w -> p t w", t=T), padding[:])\
                  .then_inc(padded, 16)
            sp.wait_ge(padded, 16 * (2 * E - 1))

            def body(j, r, before):
                at = slice(j, j + 1) if j.__class__ is int else bass.ds(j, 1)
                wait(sp, result_done, j + (1 - RING))
                sp.sem_inc(sp_passed, 1)
                wait(sp, y_done, j + (1 - RING))
                sp.sem_inc(sp_passed, 1)
                start = sp.value_load(table[0:1, 1, at], min_val=0, max_val=E * seg + (E - 2) * block_w)
                sp.dma_start(rows[r][:], rows_dram[bass.ds(start, block_w), :].rearrange("(t p) w -> p t w", p=P))\
                  .then_inc(rows_in[r], 16)
                e = sp.value_load(table[0:1, 0, at], min_val=0, max_val=E - 1)
                one = bass.ds(e, 1)
                sp.dma_start(w1[r][:], io.W1[one].rearrange("a p f -> p (a f)")).then_inc(weights_in[r], 16)
                sp.dma_start(w2[r][:], io.W2[one].rearrange("a (f p) d -> p (a f) d", p=P)).then_inc(weights_in[r], 16)
                sp.dma_start(biases[r][:], biases_all[:, one, :]).then_inc(weights_in[r], 16)

            blocks(nc.sync, body)

        @block.tensor
        def _(pe):
            def turn(j, r, arrived):
                pe.wait_ge(rows_in[r], 16 * arrived)
                wait(pe, xt_done, j)
                for t in range(T):
                    mm = pe.transpose(ps_a[:, t * P:(t + 1) * P], rows[r][:, t, 0:D], ident[:])
                mm.then_inc(xt_mm, 1)

            def layer1(j, r, arrived):
                pe.wait_ge(weights_in[r], 48 * arrived)
                pe.wait_ge(xt_done, j + 1)
                for f in range(FT):
                    wait(pe, hid_done, (j - 1) * FT + f + 1)
                    pe.matmul(ps_f[:, f, :], w1[r][:, f * P:(f + 1) * P], x_t[r][:], start=True, stop=True).then_inc(hid_mm, 1)

            def layer2(j, r, before):
                wait(pe, y_done, j)
                for f in range(FT):
                    if f == FT // 2 and (j.__class__ is not int or j < NB - 1):
                        turn(j + 1, (r + 1) % RING, before + 1 + (r == RING - 1))
                    pe.wait_ge(hid_done, j * FT + f + 1)
                    mm = pe.matmul(ps_y[:], w2[r][:, f, :], hid[r][:, f, :], start=(f == 0), stop=(f == FT - 1))
                mm.then_inc(y_mm, 1)

            def back(j, r):
                pe.wait_ge(y_done, j + 1)
                wait(pe, r_done, j)
                for t in range(T):
                    mm = pe.transpose(ps_b[:, t * P:(t + 1) * P], y_t[r][:, t * P:(t + 1) * P], ident[:])
                mm.then_inc(back_mm, 1)

            def body(j, r, before):
                layer1(j, r, before + 1)
                if j.__class__ is not int or j > 0:
                    back(j - 1, (r - 1) % RING)
                layer2(j, r, before)

            turn(0, 0, 1)
            blocks(nc.tensor, body)
            back(NB - 1, 0)

        @block.scalar
        def _(act):
            def inputs(j, r):
                act.wait_ge(xt_mm, j + 1)
                wait(act, hid_mm, (j - 1) * FT)
                act.activation(x_t[r][:], ps_a[:], ACT.Copy).then_inc(xt_done, 1)

            def middle(j, r):
                for f in range(FT):
                    act.wait_ge(hid_mm, j * FT + f + 1)
                    if f == 0:
                        wait(act, y_mm, j - 1)
                    act.activation(hid[r][:, f, :], ps_f[:, f, :], ACT.Relu, bias=biases[r][:, 0, f:f + 1]).then_inc(hid_done, 1)

            def end(j, r):
                act.wait_ge(y_mm, j + 1)
                wait(act, back_mm, j - 1)
                act.activation(y_t[r][:], ps_y[:], ACT.Identity, bias=biases[r][:, 0, FT:FT + 1]).then_inc(y_done, 1)

            def body(j, r, before):
                act.wait_ge(weights_in[r], 48 * (before + 1))
                middle(j, r)
                if j.__class__ is not int or j < NB - 1:
                    inputs(j + 1, (r + 1) % RING)
                end(j, r)

            inputs(0, 0)
            blocks(nc.scalar, body)

        @block.vector
        def _(dve):
            def chain(ins):
                ins.then_inc(step, 1)
                chain.n += 1
                dve.wait_ge(step, chain.n)
            chain.n = 0
            dve.wait_ge(consts, 6)
            dve.tensor_copy(count_i[:], count[:]).then_inc(consts, 1)
            chain(dve.tensor_tensor(filled[:], count[:], seg_start[:], ALU.subtract))
            chain(dve.tensor_scalar(blocks_i[:, 0, :], filled[:], float(block_w - 1), None, ALU.add))
            chain(dve.tensor_scalar(blocks_i[:, 1, :], blocks_i[:, 0, :], -block_w, None, ALU.bitwise_and))
            chain(dve.tensor_scalar(n_blocks[:], blocks_i[:, 1, :], 1.0 / block_w, None, ALU.mult))
            chain(dve.tensor_copy(ends[:, 0:1], n_blocks[:, 0:1]))
            for e in range(1, E):
                chain(dve.tensor_tensor(ends[:, e:e + 1], ends[:, e - 1:e], n_blocks[:, e:e + 1], ALU.add))
            chain(dve.tensor_tensor(passed_e[:], block_no[:].rearrange("p (n a) -> p n a", a=1).broadcast_to([P, NB, E]),
                                    ends[:].rearrange("p (a e) -> p a e", a=1).broadcast_to([P, NB, E]), ALU.is_ge))
            chain(dve.tensor_reduce(expert[:], passed_e[:], AX.X, ALU.add))
            chain(dve.tensor_tensor(passed_e[:], passed_e[:], n_blocks[:].rearrange("p (a e) -> p a e", a=1)
                                    .broadcast_to([P, NB, E]), ALU.mult))
            chain(dve.tensor_reduce(first[:], passed_e[:], AX.X, ALU.add))
            chain(dve.tensor_tensor(work[:, 0, :], block_no[:], first[:], ALU.subtract))
            chain(dve.tensor_scalar(work[:, 1, :], work[:, 0, :], float(block_w), None, ALU.mult))
            chain(dve.tensor_scalar(work[:, 2, :], expert[:], float(seg), None, ALU.mult))
            chain(dve.tensor_tensor(table[:, 1, :], work[:, 1, :], work[:, 2, :], ALU.add))
            dve.wait_ge(consts, 7)
            dve.tensor_scalar(table[:, 0, :], expert[:], float(E - 1), None, ALU.min).then_inc(table_done, 1)

            def passed():
                dve.sem_inc(dve_passed, 1)

            def body(j, r, before):
                dve.wait_ge(back_mm, j + 1)
                wait(dve, sent[r], before * (16 * T))
                passed()
                dve.tensor_copy(ids[r][:], rows[r][:, :, 2 * D]).then_inc(ids_done, 1)
                wait(dve, tn_done, T * j)
                dve.tensor_tensor(r_in[:], rows[r][:, :, 0:D], ps_b[:].rearrange("p (t d) -> p t d", d=D), ALU.add)\
                   .then_inc(r_done, 1)
                dve.wait_ge(r_done, j + 1)
                for t in range(T):
                    dve.bn_stats(stats[:, t, :], r_in[:, t, :]).then_inc(stat_done, 1)
                dve.wait_ge(stat_done, T * (j + 1))
                passed()
                for t in range(T):
                    dve.bn_aggr(mv[:, t, :], stats[:, t, :]).then_inc(mean_done, 1)
                dve.wait_ge(mean_done, T * (j + 1))
                dve.tensor_scalar(vareps[:], mv[:, :, 1], EPS, None, ALU.add).then_inc(vareps_done, 1)
                dve.wait_ge(rstd_done, j + 1)
                wait(dve, result_done, j)
                for t in range(T):
                    dve.tensor_scalar(tn[:, t, :], r_in[:, t, :], mv[:, t, 0:1], rstd[:, t:t + 1],
                                      ALU.subtract, ALU.mult).then_inc(tn_done, 1)
                dve.wait_ge(tn_done, T * (j + 1))
                dve.tensor_tensor(tn[:], tn[:], bcast(ln_gb[:, 0, :]), ALU.mult).then_inc(affine, 1)
                dve.wait_ge(affine, 2 * j + 1)
                dve.tensor_tensor(tn[:], tn[:], bcast(ln_gb[:, 1, :]), ALU.add).then_inc(affine, 1)
                dve.wait_ge(affine, 2 * j + 2)
                dve.tensor_tensor(result[r][:], tn[:], rows[r][:, :, D:2 * D], ALU.add).then_inc(result_done, 1)

            blocks(nc.vector, body)


def program(nc, io, out):
    B, S, D = io.x.shape
    E = io.W1.shape[0]
    TILES = B * S // P
    BLOCK_W = 512
    ROW_W = 2 * D + 4
    SEG = B * S + BLOCK_W
    with ExitStack() as ctx:
        ident = ctx.enter_context(nc.sbuf_tensor("ident", [P, P], F32))
        ones = ctx.enter_context(nc.sbuf_tensor("ones", [P, P], F32))
        count = ctx.enter_context(nc.sbuf_tensor("count", [P, E], F32))
        passed_by = [ctx.enter_context(nc.semaphore(f"{engine}_passed")) for engine in ("sp", "pool", "dve")]
        rows_dram = nc.dram_tensor("rows", (E * SEG + (E - 1) * BLOCK_W, ROW_W), F32, kind="Internal").ap()
        ln_gb = ctx.enter_context(nc.sbuf_tensor("ln_gb", [P, 2, D], F32))
        FT = io.W1.shape[2] // P
        biases_all = ctx.enter_context(nc.sbuf_tensor("biases_all", [P, E, FT + 1], F32))
        with ExitStack() as tokens:
            x_tok = tokens.enter_context(nc.sbuf_tensor("x_tok", [P, TILES, D], F32))
            vg_t = tokens.enter_context(nc.sbuf_tensor("vg_t", [P, B, S], F32))
            wq, wk, wv, wo = (tokens.enter_context(nc.sbuf_tensor(n, [P, D], F32)) for n in ("wq", "wk", "wv", "wo"))
            bqk, rows_b, router_b = (tokens.enter_context(nc.sbuf_tensor(n, shape, F32))
                                     for n, shape in (("bqk", [P, 2]), ("rows_b", [P, 5, D]), ("router_b", [P, 1])))
            params_in = tokens.enter_context(nc.semaphore("params_in"))

            heads, tiles, head_w = N_HEAD, S // P, D // N_HEAD
            ks = [tokens.enter_context(nc.sbuf_tensor(f"ks{r}", [P, heads, S], BF16)) for r in range(2)]
            vaug = [tokens.enter_context(nc.sbuf_tensor(f"vaug{r}", [P, tiles, heads, VALUE_W], F32)) for r in range(2)]
            minus = tokens.enter_context(nc.sbuf_tensor("minus", [SPLIT, S], BF16))
            set_up = tokens.enter_context(nc.semaphore("set_up"))
            zeroed = tokens.enter_context(nc.semaphore("zeroed"))

            def later_constants(pool):
                pool.memset(minus[:], -1.0).then_inc(zeroed, 1)
                for r in range(2):
                    pool.memset(ks[r][:].rearrange("p h t -> p (h t)").bitcast(F32), 0.0).then_inc(zeroed, 1)
                for r in range(2):
                    pool.memset(vaug[r][:], 0.0).then_inc(zeroed, 1)
                pool.wait_ge(zeroed, 5)
                for r in range(2):
                    pool.memset(vaug[r][:, :, :, head_w:head_w + 1], 1.0).then_inc(set_up, 1)

            def later_loads(sp):
                for n, w in enumerate((io.Wq, io.Wk, io.Wv, io.Wo)):
                    sp.dma_start((wq, wk, wv, wo)[n][:], w).then_inc(params_in, 16)
                sp.dma_start(bqk[:, 0:1], column(io.bq)).then_inc(params_in, 16)
                sp.dma_start(bqk[:, 1:2], column(io.bk)).then_inc(params_in, 16)
                for n, w in enumerate((io.bv, io.bo, io.ln1_g, io.ln1_b)):
                    sp.dma_start(rows_b[:, n, :], on_all(w, D)).then_inc(params_in, 16)
                sp.dma_start(rows_b[:, 4, :], io.router_w.rearrange("d a -> a d").broadcast_to([P, D])).then_inc(params_in, 16)
                sp.dma_start(router_b[:], on_all(io.router_b, 1)).then_inc(params_in, 16)
                sp.dma_start(ln_gb[:, 0, :], on_all(io.ln2_g, D)).then_inc(params_in, 16)
                sp.dma_start(ln_gb[:, 1, :], on_all(io.ln2_b, D)).then_inc(params_in, 16)
                for e in range(E):
                    sp.dma_start(biases_all[:, e, 0:FT], io.b1[e].rearrange("(f p) -> p f", p=P),
                                 allow_slow_non_contiguous=True).then_inc(params_in, 16)
                    sp.dma_start(biases_all[:, e, FT:FT + 1], column(io.b2[e])).then_inc(params_in, 16)
                sp.wait_ge(zeroed, 3)
                first = 2 * PRODUCTS * head_w
                for r in range(2):
                    for hh in range(2):
                        own = ks[r][:].rearrange("p (pr hh) t -> p pr hh t", hh=2)
                        sp.dma_start(own[first + SPLIT * hh:first + SPLIT * (hh + 1), :, hh, :],
                                     minus[:].rearrange("p (a t) -> p a t", a=1).broadcast_to([SPLIT, heads // 2, S]))\
                          .then_inc(set_up, 16)

            memory_program(nc, io, x_tok, vg_t, ident, ones, later_loads, later_constants)
            attention_program(nc, io, x_tok, vg_t, ident, ones, rows_dram, SEG, ROW_W, count, passed_by,
                              (wq, wk, wv, wo, bqk, rows_b, router_b, params_in, ks, vaug, set_up))
        experts_program(nc, io, ident, rows_dram, SEG, ROW_W, BLOCK_W, count, passed_by, ln_gb, biases_all, out)


def kernel(**inputs):
    import numpy as np
    import concourse.bacc as bacc
    from concourse.bass_utils import run_bass_kernel_spmd

    nc = bacc.Bacc("TRN2", target_bir_lowering=False, num_devices=1)
    arrays, aps = {}, []
    for name in ["L0_attn_" + n for n in _ATTN] + ["L0_ffn_" + n for n in _FFN]:
        a = np.ascontiguousarray(inputs[name])
        arrays[f"in_{name}"] = a
        aps.append(nc.dram_tensor(f"in_{name}", a.shape, mybir.dt.from_np(a.dtype), kind="ExternalInput").ap())
    out = nc.dram_tensor("out_0", inputs["L0_attn_x"].shape, F32, kind="ExternalOutput").ap()
    program(nc, Inputs(*aps), out)
    return run_bass_kernel_spmd(nc, [arrays], core_ids=[0]).results[0]["out_0"]
```
